# Optimizing a Trainium2 kernel written in Bass

```python
import numpy as np
import jax
import jax.numpy as jnp

def _softmax(x, axis=-1):
    return jax.nn.softmax(x, axis=axis)

def _gelu(x):
    return jax.nn.gelu(x, approximate=True)

def _silu(x):
    return jax.nn.silu(x)

def _sigmoid(x):
    return jax.nn.sigmoid(x)

def _layernorm(x, axis=-1, eps=1e-05):
    m = jnp.mean(x, axis=axis, keepdims=True)
    v = jnp.var(x, axis=axis, keepdims=True)
    return (x - m) / jnp.sqrt(v + eps)

def _scatter_add(tgt, idx, src, axis=0):
    return tgt.at[idx].add(src)

def _segment_sum(src, seg, n):
    return jax.ops.segment_sum(src, seg, n)
kernel_name = 'mk_audio_tower_d1_tok_audfeat256_r4_bf75f8'

def setup_inputs(seed: int=0):
    np.random.seed(seed)
    _w = jnp.asarray

    def _rec_inputs():
        import jax
        import jax.numpy as jnp
        _rk = jax.random.key(seed)
        x = -0.000520686 + 1.00062 * jax.random.normal(jax.random.fold_in(_rk, 1), (64, 750, 64), jnp.float32)
        return x
    x = _rec_inputs()

    def _L0_tok_setup():
        import jax, jax.numpy as jnp
        import numpy as np
        BATCH = 2
        SEQ = 1024
        D_MODEL = 64
        N_STATE = 64
        DT_RANK = 1
        NUM_LAYERS = 3

        def _ssm_layer(x, A_log, Dp, W_dbc, W_dt, b_dt):
            A = -jnp.exp(A_log)
            dbc = jnp.einsum('ble,ce->blc', x, W_dbc)
            delta, Bm, Cm = jnp.split(dbc, [DT_RANK, DT_RANK + N_STATE], axis=-1)
            delta = jax.nn.softplus(jnp.einsum('blr,er->ble', delta, W_dt) + b_dt)
            dA = jnp.exp(delta[..., None] * A)
            dBx = (delta * x)[..., None] * Bm[:, :, None, :]

            def combine(c1, c2):
                a1, h1 = c1
                a2, h2 = c2
                return (a1 * a2, h1 * a2 + h2)
            _, hs = jax.lax.associative_scan(combine, (dA, dBx), axis=1)
            y = jnp.einsum('blen,bln->ble', hs, Cm)
            return y + Dp * x
        key = jax.random.key(seed)
        kx, kw1, kw2 = jax.random.split(key, 3)
        x = jax.random.normal(kx, (BATCH, SEQ, D_MODEL), dtype=jnp.float32)
        A_log = jnp.broadcast_to(jnp.log(jnp.arange(1, N_STATE + 1, dtype=jnp.float32)), (NUM_LAYERS, D_MODEL, N_STATE)).copy()
        D = jnp.ones((NUM_LAYERS, D_MODEL), dtype=jnp.float32)
        W_dbc = 0.02 * jax.random.normal(kw1, (NUM_LAYERS, DT_RANK + 2 * N_STATE, D_MODEL), dtype=jnp.float32)
        W_dt = 0.02 * jax.random.normal(kw2, (NUM_LAYERS, D_MODEL, DT_RANK), dtype=jnp.float32)
        b_dt = jnp.zeros((NUM_LAYERS, D_MODEL), dtype=jnp.float32)
        return {'x': x, 'A_log': A_log, 'D': D, 'W_dbc': W_dbc, 'W_dt': W_dt, 'b_dt': b_dt}
    _L0_tok_all = _L0_tok_setup()
    _L0_tok_in = {k: v for k, v in _L0_tok_all.items() if k in ('A_log', 'D', 'W_dbc', 'W_dt', 'b_dt')}
    del _L0_tok_all

    def _L0_attn_setup():
        import jax, jax.numpy as jnp
        import numpy as np
        B, T, D = (4, 512, 64)
        W_LORA, A_LORA, G_LORA = (64, 64, 128)
        DECAY_SCALE = -0.6065306597126334
        EPS = D * 1e-05

        def _forward(x, x_mix, W_r, W_k, W_v, W_o, A_w, B_w, b_w, A_a, B_a, b_a, A_g, B_g, k_k, k_a, r_k, gn_w, gn_b):
            b, t, d = x.shape
            shifted = jnp.pad(x, ((0, 0), (1, 0), (0, 0)))[:, :-1]
            delta = shifted - x
            xr, xw, xk, xv, xa, xg = [x + delta * x_mix[i] for i in range(6)]
            r = xr @ W_r
            w = DECAY_SCALE * jax.nn.sigmoid(jnp.tanh(xw @ A_w) @ B_w + b_w)
            k = xk @ W_k
            v = xv @ W_v
            a = jax.nn.sigmoid(xa @ A_a @ B_a + b_a)
            g = jax.nn.sigmoid(xg @ A_g) @ B_g
            kk = k * k_k
            kk = kk / jnp.maximum(jnp.linalg.norm(kk, axis=-1, keepdims=True), 1e-12)
            k = k * (1.0 + (a - 1.0) * k_a)
            decay = jnp.exp(w)

            def step(S, inp):
                r_t, dec_t, k_t, v_t, kk_t, a_t = inp
                b_t = kk_t * a_t
                sa = jnp.einsum('bvk,bk->bv', S, -kk_t)
                S = S * dec_t[:, None, :] + sa[:, :, None] * b_t[:, None, :] + v_t[:, :, None] * k_t[:, None, :]
                o_t = jnp.einsum('bvk,bk->bv', S, r_t)
                return (S, o_t)
            tm = lambda z: jnp.swapaxes(z, 0, 1)
            S0 = jnp.zeros((b, d, d), x.dtype)
            _, o = jax.lax.scan(step, S0, (tm(r), tm(decay), tm(k), tm(v), tm(kk), tm(a)))
            o = jnp.swapaxes(o, 0, 1)
            mu = jnp.mean(o, axis=-1, keepdims=True)
            var = jnp.var(o, axis=-1, keepdims=True)
            o = (o - mu) * jax.lax.rsqrt(var + EPS) * gn_w + gn_b
            o = o + jnp.sum(r * k * r_k, axis=-1, keepdims=True) * v
            return o * g @ W_o
        key = jax.random.key(seed)
        ks = jax.random.split(key, 20)
        n = jax.random.normal
        p = {}
        p['x'] = n(ks[0], (B, T, D), jnp.float32)
        p['x_mix'] = n(ks[1], (6, D), jnp.float32) * 0.1
        s = 1.0 / np.sqrt(D).astype(np.float32)
        p['W_r'] = n(ks[2], (D, D), jnp.float32) * s
        p['W_k'] = n(ks[3], (D, D), jnp.float32) * s
        p['W_v'] = n(ks[4], (D, D), jnp.float32) * s
        p['W_o'] = n(ks[5], (D, D), jnp.float32) * s
        p['A_w'] = n(ks[6], (D, W_LORA), jnp.float32) * s
        p['B_w'] = n(ks[7], (W_LORA, D), jnp.float32) / np.sqrt(W_LORA).astype(np.float32)
        p['b_w'] = n(ks[8], (D,), jnp.float32) * 0.5
        p['A_a'] = n(ks[9], (D, A_LORA), jnp.float32) * s
        p['B_a'] = n(ks[10], (A_LORA, D), jnp.float32) / np.sqrt(A_LORA).astype(np.float32)
        p['b_a'] = n(ks[11], (D,), jnp.float32) * 0.1
        p['A_g'] = n(ks[12], (D, G_LORA), jnp.float32) * s
        p['B_g'] = n(ks[13], (G_LORA, D), jnp.float32) / np.sqrt(G_LORA).astype(np.float32)
        p['k_k'] = n(ks[14], (D,), jnp.float32) * 0.5 + 0.85
        p['k_a'] = n(ks[15], (D,), jnp.float32) * 0.1 + 1.0
        p['r_k'] = n(ks[16], (D,), jnp.float32) * 0.1
        p['gn_w'] = jnp.ones((D,), jnp.float32)
        p['gn_b'] = jnp.zeros((D,), jnp.float32)
        return p
    _L0_attn_all = _L0_attn_setup()
    _L0_attn_in = {k: v for k, v in _L0_attn_all.items() if k in ('x_mix', 'W_r', 'W_k', 'W_v', 'W_o', 'A_w', 'B_w', 'b_w', 'A_a', 'B_a', 'b_a', 'A_g', 'B_g', 'k_k', 'k_a', 'r_k', 'gn_w', 'gn_b')}
    del _L0_attn_all

    def _L0_ffn_setup():
        import jax, jax.numpy as jnp
        import numpy as np
        BN_EPS = 0.001

        def _bn(h, g, b, m, v):
            return g * (h - m) * jax.lax.rsqrt(v + BN_EPS) + b
        key = jax.random.key(seed)
        ks = jax.random.split(key, 8)
        B, F, Df = (64, 64, 64)
        E, H, D = (8, 64, 64)
        s1 = 1.0 / np.sqrt(Df)
        s2 = 1.0 / np.sqrt(H)
        return {'x': jax.random.normal(ks[0], (B, F, Df), jnp.float32), 'Wr': jax.random.normal(ks[1], (Df, E), jnp.float32) * s1, 'br': jnp.zeros((E,), jnp.float32), 'W1': jax.random.normal(ks[2], (E, Df, H), jnp.float32) * s1, 'b1': jnp.zeros((E, H), jnp.float32), 'g1': jnp.ones((E, H), jnp.float32), 'be1': jnp.zeros((E, H), jnp.float32), 'm1': jnp.zeros((E, H), jnp.float32), 'v1': jnp.ones((E, H), jnp.float32), 'W2': jax.random.normal(ks[3], (E, H, H), jnp.float32) * s2, 'b2': jnp.zeros((E, H), jnp.float32), 'g2': jnp.ones((E, H), jnp.float32), 'be2': jnp.zeros((E, H), jnp.float32), 'm2': jnp.zeros((E, H), jnp.float32), 'v2': jnp.ones((E, H), jnp.float32), 'Wo': jax.random.normal(ks[4], (E, H, D), jnp.float32) * s2, 'bo': jnp.zeros((E, D), jnp.float32)}
    _L0_ffn_all = _L0_ffn_setup()
    _L0_ffn_in = {k: v for k, v in _L0_ffn_all.items() if k in ('Wr', 'br', 'W1', 'b1', 'g1', 'be1', 'm1', 'v1', 'W2', 'b2', 'g2', 'be2', 'm2', 'v2', 'Wo', 'bo')}
    del _L0_ffn_all
    return {'x': x, 'L0_tok_A_log': _L0_tok_in['A_log'], 'L0_tok_D': _L0_tok_in['D'], 'L0_tok_W_dbc': _L0_tok_in['W_dbc'], 'L0_tok_W_dt': _L0_tok_in['W_dt'], 'L0_tok_b_dt': _L0_tok_in['b_dt'], 'L0_attn_x_mix': _L0_attn_in['x_mix'], 'L0_attn_W_r': _L0_attn_in['W_r'], 'L0_attn_W_k': _L0_attn_in['W_k'], 'L0_attn_W_v': _L0_attn_in['W_v'], 'L0_attn_W_o': _L0_attn_in['W_o'], 'L0_attn_A_w': _L0_attn_in['A_w'], 'L0_attn_B_w': _L0_attn_in['B_w'], 'L0_attn_b_w': _L0_attn_in['b_w'], 'L0_attn_A_a': _L0_attn_in['A_a'], 'L0_attn_B_a': _L0_attn_in['B_a'], 'L0_attn_b_a': _L0_attn_in['b_a'], 'L0_attn_A_g': _L0_attn_in['A_g'], 'L0_attn_B_g': _L0_attn_in['B_g'], 'L0_attn_k_k': _L0_attn_in['k_k'], 'L0_attn_k_a': _L0_attn_in['k_a'], 'L0_attn_r_k': _L0_attn_in['r_k'], 'L0_attn_gn_w': _L0_attn_in['gn_w'], 'L0_attn_gn_b': _L0_attn_in['gn_b'], 'L0_ffn_Wr': _L0_ffn_in['Wr'], 'L0_ffn_br': _L0_ffn_in['br'], 'L0_ffn_W1': _L0_ffn_in['W1'], 'L0_ffn_b1': _L0_ffn_in['b1'], 'L0_ffn_g1': _L0_ffn_in['g1'], 'L0_ffn_be1': _L0_ffn_in['be1'], 'L0_ffn_m1': _L0_ffn_in['m1'], 'L0_ffn_v1': _L0_ffn_in['v1'], 'L0_ffn_W2': _L0_ffn_in['W2'], 'L0_ffn_b2': _L0_ffn_in['b2'], 'L0_ffn_g2': _L0_ffn_in['g2'], 'L0_ffn_be2': _L0_ffn_in['be2'], 'L0_ffn_m2': _L0_ffn_in['m2'], 'L0_ffn_v2': _L0_ffn_in['v2'], 'L0_ffn_Wo': _L0_ffn_in['Wo'], 'L0_ffn_bo': _L0_ffn_in['bo']}

def reference(x, L0_tok_A_log, L0_tok_D, L0_tok_W_dbc, L0_tok_W_dt, L0_tok_b_dt, L0_attn_x_mix, L0_attn_W_r, L0_attn_W_k, L0_attn_W_v, L0_attn_W_o, L0_attn_A_w, L0_attn_B_w, L0_attn_b_w, L0_attn_A_a, L0_attn_B_a, L0_attn_b_a, L0_attn_A_g, L0_attn_B_g, L0_attn_k_k, L0_attn_k_a, L0_attn_r_k, L0_attn_gn_w, L0_attn_gn_b, L0_ffn_Wr, L0_ffn_br, L0_ffn_W1, L0_ffn_b1, L0_ffn_g1, L0_ffn_be1, L0_ffn_m1, L0_ffn_v1, L0_ffn_W2, L0_ffn_b2, L0_ffn_g2, L0_ffn_be2, L0_ffn_m2, L0_ffn_v2, L0_ffn_Wo, L0_ffn_bo):
    import jax
    import jax.numpy as jnp

    def _L0_tok_ref(x, A_log, D, W_dbc, W_dt, b_dt):
        import jax, jax.numpy as jnp
        import numpy as np
        BATCH = 2
        SEQ = 1024
        D_MODEL = 64
        N_STATE = 64
        DT_RANK = 1
        NUM_LAYERS = 3

        def _ssm_layer(x, A_log, Dp, W_dbc, W_dt, b_dt):
            A = -jnp.exp(A_log)
            dbc = jnp.einsum('ble,ce->blc', x, W_dbc)
            delta, Bm, Cm = jnp.split(dbc, [DT_RANK, DT_RANK + N_STATE], axis=-1)
            delta = jax.nn.softplus(jnp.einsum('blr,er->ble', delta, W_dt) + b_dt)
            dA = jnp.exp(delta[..., None] * A)
            dBx = (delta * x)[..., None] * Bm[:, :, None, :]

            def combine(c1, c2):
                a1, h1 = c1
                a2, h2 = c2
                return (a1 * a2, h1 * a2 + h2)
            _, hs = jax.lax.associative_scan(combine, (dA, dBx), axis=1)
            y = jnp.einsum('blen,bln->ble', hs, Cm)
            return y + Dp * x
        for i in range(NUM_LAYERS):
            x = _ssm_layer(x, A_log[i], D[i], W_dbc[i], W_dt[i], b_dt[i])
            if i < NUM_LAYERS - 1:
                b, l, d = x.shape
                x = x[:, :l // 2 * 2].reshape(b, l // 2, 2, d).mean(axis=2)
        return x

    def _L0_attn_ref(x, x_mix, W_r, W_k, W_v, W_o, A_w, B_w, b_w, A_a, B_a, b_a, A_g, B_g, k_k, k_a, r_k, gn_w, gn_b):
        import jax, jax.numpy as jnp
        import numpy as np
        B, T, D = (4, 512, 64)
        W_LORA, A_LORA, G_LORA = (64, 64, 128)
        DECAY_SCALE = -0.6065306597126334
        EPS = D * 1e-05

        def _forward(x, x_mix, W_r, W_k, W_v, W_o, A_w, B_w, b_w, A_a, B_a, b_a, A_g, B_g, k_k, k_a, r_k, gn_w, gn_b):
            b, t, d = x.shape
            shifted = jnp.pad(x, ((0, 0), (1, 0), (0, 0)))[:, :-1]
            delta = shifted - x
            xr, xw, xk, xv, xa, xg = [x + delta * x_mix[i] for i in range(6)]
            r = xr @ W_r
            w = DECAY_SCALE * jax.nn.sigmoid(jnp.tanh(xw @ A_w) @ B_w + b_w)
            k = xk @ W_k
            v = xv @ W_v
            a = jax.nn.sigmoid(xa @ A_a @ B_a + b_a)
            g = jax.nn.sigmoid(xg @ A_g) @ B_g
            kk = k * k_k
            kk = kk / jnp.maximum(jnp.linalg.norm(kk, axis=-1, keepdims=True), 1e-12)
            k = k * (1.0 + (a - 1.0) * k_a)
            decay = jnp.exp(w)

            def step(S, inp):
                r_t, dec_t, k_t, v_t, kk_t, a_t = inp
                b_t = kk_t * a_t
                sa = jnp.einsum('bvk,bk->bv', S, -kk_t)
                S = S * dec_t[:, None, :] + sa[:, :, None] * b_t[:, None, :] + v_t[:, :, None] * k_t[:, None, :]
                o_t = jnp.einsum('bvk,bk->bv', S, r_t)
                return (S, o_t)
            tm = lambda z: jnp.swapaxes(z, 0, 1)
            S0 = jnp.zeros((b, d, d), x.dtype)
            _, o = jax.lax.scan(step, S0, (tm(r), tm(decay), tm(k), tm(v), tm(kk), tm(a)))
            o = jnp.swapaxes(o, 0, 1)
            mu = jnp.mean(o, axis=-1, keepdims=True)
            var = jnp.var(o, axis=-1, keepdims=True)
            o = (o - mu) * jax.lax.rsqrt(var + EPS) * gn_w + gn_b
            o = o + jnp.sum(r * k * r_k, axis=-1, keepdims=True) * v
            return o * g @ W_o
        return _forward(x, x_mix, W_r, W_k, W_v, W_o, A_w, B_w, b_w, A_a, B_a, b_a, A_g, B_g, k_k, k_a, r_k, gn_w, gn_b)

    def _L0_ffn_ref(x, Wr, br, W1, b1, g1, be1, m1, v1, W2, b2, g2, be2, m2, v2, Wo, bo):
        import jax, jax.numpy as jnp
        import numpy as np
        BN_EPS = 0.001

        def _bn(h, g, b, m, v):
            return g * (h - m) * jax.lax.rsqrt(v + BN_EPS) + b
        feat = jnp.mean(x, axis=0)
        w = jax.nn.softmax(feat @ Wr + br, axis=-1)
        h = jnp.einsum('bfd,edh->bfeh', x, W1) + b1
        h = jax.nn.relu(_bn(h, g1, be1, m1, v1))
        h = jnp.einsum('bfeh,ehk->bfek', h, W2) + b2
        h = jax.nn.relu(_bn(h, g2, be2, m2, v2))
        y = jnp.einsum('bfeh,ehd->bfed', h, Wo) + bo
        return jnp.einsum('bfed,fe->bfd', y, w)
    h = _L0_tok_ref(x, L0_tok_A_log, L0_tok_D, L0_tok_W_dbc, L0_tok_W_dt, L0_tok_b_dt)
    h = h + _L0_attn_ref(_layernorm(h, axis=-1), L0_attn_x_mix, L0_attn_W_r, L0_attn_W_k, L0_attn_W_v, L0_attn_W_o, L0_attn_A_w, L0_attn_B_w, L0_attn_b_w, L0_attn_A_a, L0_attn_B_a, L0_attn_b_a, L0_attn_A_g, L0_attn_B_g, L0_attn_k_k, L0_attn_k_a, L0_attn_r_k, L0_attn_gn_w, L0_attn_gn_b)
    h = h + _L0_ffn_ref(_layernorm(h, axis=-1), L0_ffn_Wr, L0_ffn_br, L0_ffn_W1, L0_ffn_b1, L0_ffn_g1, L0_ffn_be1, L0_ffn_m1, L0_ffn_v1, L0_ffn_W2, L0_ffn_b2, L0_ffn_g2, L0_ffn_be2, L0_ffn_m2, L0_ffn_v2, L0_ffn_Wo, L0_ffn_bo)
    return h

_drawn_inputs = setup_inputs


def setup_inputs(seed=0):
    import zlib

    import numpy as np

    out = dict(_drawn_inputs(seed))
    spreads = {'L0_tok_D': (1.0, 0.2),
     'L0_tok_b_dt': (0.0, 0.412),
     'L0_attn_gn_w': (1.0, 0.2),
     'L0_attn_gn_b': (0.0, 0.1),
     'L0_ffn_br': (0.0, 0.1),
     'L0_ffn_b1': (0.0, 0.354),
     'L0_ffn_g1': (1.0, 0.2),
     'L0_ffn_be1': (0.0, 0.338),
     'L0_ffn_m1': (0.0, 0.364),
     'L0_ffn_v1': (1.0, 0.6),
     'L0_ffn_b2': (0.0, 0.1),
     'L0_ffn_g2': (1.0, 0.2),
     'L0_ffn_be2': (0.0, 0.289),
     'L0_ffn_m2': (0.0, 0.1),
     'L0_ffn_v2': (1.0, 0.6),
     'L0_ffn_bo': (0.0, 0.1)}
    factors = {'L0_tok_A_log': 15.066, 'L0_tok_W_dt': 64.0}
    for name, (base, spread) in spreads.items():
        noise = np.random.default_rng([zlib.crc32(name.encode()), seed]).standard_normal(out[name].shape)
        drawn = base * np.exp(spread * noise) if base else spread * noise
        out[name] = jnp.asarray(drawn.astype(out[name].dtype))
    for name, factor in factors.items():
        out[name] = (out[name] * factor).astype(out[name].dtype)
    return out
```

```python
from contextlib import ExitStack

import concourse.bass as bass
from concourse import mybir

ALU = mybir.AluOpType
ACT = mybir.ActivationFunctionType
F32 = mybir.dt.float32
BF16 = mybir.dt.bfloat16
AX_X = mybir.AxisListType.X

P = 128
D = 64
T = [750, 375, 187]
Q = 8
TQ = [-(-t // Q) for t in T]
EG = 16
NG = D // EG
PAIRS = 32
HALF = PAIRS // 2
ITEMS = [(a, l) for l in range(3) for a in range(2)]
NI = len(ITEMS)
WIDE = 375
STREAM = 96
NSPLIT = 24


def halves(l):
    return [(c, min(c + WIDE, T[l])) for c in range(0, T[l], WIDE)]


def pieces(l):
    n = TQ[l]
    parts = -(-n // 32)
    step = -(-n // parts)
    return [(k, min(k + step, n)) for k in range(0, n, step)]


def k_slots(l, slots):
    parts = pieces(l)
    per = -(-(parts[0][1] - parts[0][0]) // (slots // len(parts)))
    out = [[] for _ in range(EG)]
    slot = 1
    for j, (a, b) in enumerate(parts):
        for k in range(a, b, per):
            out[slot].append((j, k, min(k + per, b)))
            slot += 1
    return out


def evac_slots(l, slots):
    last = {}
    for e, todo in enumerate(k_slots(l, slots)):
        for j, _, _ in todo:
            last[j] = e
    return last


def spread(g):
    return 6 if g == NG - 1 else 12


def ybank_schedule():
    order = []
    for s, (a, l) in enumerate(ITEMS):
        for h in range(len(halves(l))):
            order.append(("c", s, h))
        if s > 0:
            for h in range(2):
                order.append(("fin", s - 1, h))
        n = (s + 1) % NI
        for w in ("z", "b"):
            for h in range(len(halves(ITEMS[n][1]))):
                order.append((w, n, h))
    for h in range(2):
        order.append(("fin", NI - 1, h))
    return {u: i for i, u in enumerate(order)}


def ssm_phase(nc, ctx, xT, A_log, Dp, Wb, Wc, Wr, Wdt, bdt, sel_d, z_d, hid):
    sb = lambda n, s, d=F32: ctx.enter_context(nc.sbuf_tensor(n, s, d))
    ps = lambda n, s, d=F32: ctx.enter_context(nc.psum_tensor(n, s, d))
    sem = lambda n: ctx.enter_context(nc.semaphore(n))

    hst = sb("hst", [P, 2, EG * Q * TQ[0]])
    osb = sb("osb", [P, NG, TQ[0] * 2 * Q])
    RD = sb("RD", [96, 2, NG, T[0]], BF16)
    RU = sb("RU", [96, 2, NG, T[0]], BF16)
    xs = [sb(f"x{l}", [P, 2, T[l]]) for l in range(3)]
    Bs = sb("Bs", [P, 2, T[0]])
    Cb = sb("Cb", [P, TQ[0] * 2 * Q + STREAM])
    ub = sb("ub", [P, 2, T[0]])
    db = sb("db", [P, 2, T[0]])
    zz = sb("zz", [P, T[0]])
    ss = sb("ss", [P, T[0]])
    dp = sb("dp", [P, 3, T[0]], BF16)
    up = sb("up", [P, 3, T[0]], BF16)
    xf = sb("xf", [P, Q * TQ[0]])
    sel = sb("sel", [96, EG, P], BF16)
    zsel = sb("zsel", [P, Q, 112])
    wb = sb("wb", [P, 3, P])
    wc = sb("wc", [P, 3, P])
    wr = sb("wr", [P, 3, P])
    A = sb("A", [P, 3, D])
    hd = sb("hd", [P, 3])
    wdt = sb("wdt", [P, 3])
    bd = sb("bd", [P, 3])

    pD = ps("pD", [P, 2, 1024])
    pU = ps("pU", [P, 1024])
    pO = ps("pO", [P, 512])
    pY = ps("pY", [P, 512])

    names = ("const", "aexp", "xload", "bcd", "bcu", "ucopy", "decay", "dbx", "scan", "ymm", "oev",
             "yfull", "cev", "bev", "zev", "zneg", "sp1", "sp", "dlt", "ux", "cast1", "res1", "cast2",
             "part", "rdl", "rul", "fin1", "fin", "hout", "mset", "selc")
    S = {n: sem("s_" + n) for n in names}
    yb = ybank_schedule()
    YN = len(yb)
    EN = NI * D
    ZN = sum(len(halves(l)) for _, l in ITEMS)
    ON = sum(len(pieces(l)) for _, l in ITEMS) * NG

    def zcount(s):
        return sum(len(halves(l)) for _, l in ITEMS[:s])

    def ocount(s, g):
        return sum(len(pieces(l)) for _, l in ITEMS[:s]) * NG + g * len(pieces(ITEMS[s][1]))

    def zdone(n, h):
        return (zcount(n) if n else ZN) + h + 1

    ZPRE = len(halves(0))

    CONSTS = [(sel, sel_d), (zsel, z_d), (wb, Wb), (wc, Wc), (wr, Wr), (A, A_log), (hd, Dp), (wdt, Wdt), (bd, bdt)]

    def full(t):
        return t[:]

    def prev_group(s, g):
        if g > 0:
            return s, g - 1
        return (s - 1, NG - 1) if s > 0 else None

    with nc.Block() as block:
        @block.sync
        def _(sp):
            for dst, src in CONSTS[1:]:
                sp.dma_start(full(dst), src).then_inc(S["const"], 16)
            sp.dma_start(hst[0:96, 0, 0:EG * P], sel_d.rearrange("k e m -> k (e m)")).then_inc(S["hout"], 16)
            sp.dma_start(xs[0][:, 0, :], xT[0, :, :]).then_inc(S["xload"], 16)

            def waits(*pairs):
                for name, value in pairs:
                    sp.wait_ge(S[name], value)
                    sp.wait_ge(S["const"], 16 * (len(CONSTS) - 1))

            def restack(i, s, l, par):
                for src, dst, done in ((dp, RD, "rdl"), (up, RU, "rul")):
                    for r in range(3):
                        for b in range(2):
                            for g in range(NG):
                                sp.dma_start(dst[32 * r + 16 * b:32 * r + 16 * b + 16, par, g, 0:T[l]],
                                             src[64 * b + 16 * g:64 * b + 16 * g + 16, r, 0:T[l]]).then_inc(S[done], 16)

            sp.wait_ge(S["part"], 2)
            restack(0, 0, 0, 0)
            with sp.Fori(0, HALF) as i:
                i_b, i_a = sp.snap(i + HALF), sp.snap(i + 1)
                waits(("fin", i * NI + 1))
                sp.dma_start(xs[0][:, 1, :], xT[bass.ds(i_b, 1), :, :].rearrange("o p t -> p (o t)"))\
                    .then_inc(S["xload"], 16)
                for s in range(NI):
                    n = (s + 1) % NI
                    nl = ITEMS[n][1]
                    if s == 2:
                        waits(("fin", i * NI + 2))
                        sp.dma_start(xs[0][:, 0, :], xT[bass.ds(i_a, 1), :, :].rearrange("o p t -> p (o t)"))\
                            .then_inc(S["xload"], 16)
                    sp.wait_ge(S["part"], i * 2 * NI + 2 * (s + 2))
                    restack(i, n, nl, n % 2)
                    if s == 5:
                        waits(("fin", i * NI + 6))
                        sp.dma_start(hid[bass.ds(i, 1), :, :].rearrange("o p t -> p (o t)"), xs[2][:, 0, :])\
                            .then_inc(S["hout"], 16)
                waits(("fin", i * NI + 7))
                sp.dma_start(hid[bass.ds(i_b, 1), :, :].rearrange("o p t -> p (o t)"), xs[2][:, 1, :])\
                    .then_inc(S["hout"], 16)
            sp.wait_ge(S["hout"], 16 * (2 * HALF + 1))

        @block.tensor
        def _(pe):
            def bank_free(i, use):
                k = yb[use]
                if k == 0:
                    pe.wait_ge(S["bev"], i * ZN + ZPRE)
                    pe.wait_ge(S["fin1"], i * 2 * NI + 1)
                    return
                kind, s, h = [u for u, n in yb.items() if n == k - 1][0]
                if kind == "c":
                    pe.wait_ge(S["cev"], i * ZN + zcount(s) + h + 1)
                elif kind == "fin":
                    pe.wait_ge(S["fin1"], i * 2 * NI + 2 * s + h + 2)
                else:
                    pe.wait_ge(S["zev" if kind == "z" else "bev"], i * ZN + zdone(s, h))

            def project(w, l, a, c0, c1):
                pe.matmul(pY[:, 0:c1 - c0], w[:, l, :], xs[l][:, a, c0:c1], start=True, stop=True)\
                    .then_inc(S["yfull"], 1)

            def y_step(i, s, g, l, todo):
                for j, k0, k1 in todo:
                    n = ocount(s, g) + j
                    if k0 == pieces(l)[0][0] and j == 0:
                        pe.wait_ge(S["scan"], i * EN + D * s + EG * (g + 1) + 2)
                        pe.wait_ge(S["cev"], i * ZN + zcount(s + 1))
                    if k0 == pieces(l)[j][0] and n > 0:
                        pe.wait_ge(S["oev"], i * ON + n)
                    par = g % 2
                    hv = hst[:, par, 0:EG * Q * TQ[l]]
                    for k in range(k0, k1):
                        c = 2 * Q * (k - pieces(l)[j][0])
                        n = min(STREAM, 512 - c)
                        last = pe.matmul(pO[:, c:c + n], hv[:, k:k + (P - 1) * TQ[l] + 1:TQ[l]],
                                         Cb[:, 2 * Q * k:2 * Q * k + n], start=True, stop=True)
                    if k1 == pieces(l)[j][1]:
                        last.then_inc(S["ymm"], 1)

            def fin_step(i, s, h, q, b):
                l = ITEMS[s][1]
                if q == 0 and b == 0:
                    bank_free(i, ("fin", s, h))
                    pe.wait_ge(S["oev"], i * ON + ocount(s, NG))
                ov = osb[:, :, 0:2 * Q * TQ[l]].rearrange("p g (k c) -> p g k c", c=2 * Q)
                col = 2 * (4 * h + q) + b
                for g in range(NG):
                    last = pe.matmul(pY[64 * b:64 * b + 64, q * TQ[l]:(q + 1) * TQ[l]],
                                     zsel[:, 4 * h + q, 48 - 16 * g:112 - 16 * g], ov[:, g, :, col],
                                     start=(g == 0), stop=(g == NG - 1))
                if q == 3 and b == 1:
                    last.then_inc(S["yfull"], 1)

            pe.wait_ge(S["const"], 16 * (len(CONSTS) - 1))
            pe.wait_ge(S["selc"], 1)
            pe.wait_ge(S["xload"], 16)
            for u, (c0, c1) in enumerate(halves(0)):
                if u:
                    pe.wait_ge(S["zev"], u)
                project(wr, 0, 0, c0, c1)
            for u, (c0, c1) in enumerate(halves(0)):
                pe.wait_ge(S["bev" if u else "zev"], u or ZPRE)
                project(wb, 0, 0, c0, c1)

            with pe.Fori(0, HALF) as i:
                for s, (a, l) in enumerate(ITEMS):
                    n = (s + 1) % NI
                    na, nl = ITEMS[n]
                    for g in range(NG):
                        for e in range(EG):
                            E = D * s + EG * g + e
                            if g == 0 and e == 0:
                                pe.wait_ge(S["rdl"], (i * NI + s + 1) * 16 * NSPLIT)
                                pe.wait_ge(S["rul"], (i * NI + s + 1) * 16 * NSPLIT)
                            pe.wait_ge(S["ucopy"], i * EN + E + 1)
                            for c0, c1 in ((0, min(512, T[l])), (512, T[l])):
                                if c1 > c0:
                                    last = pe.matmul(pU[:, c0:c1], sel[:, e, :], RU[:, s % 2, g, c0:c1],
                                                     start=True, stop=True)
                            last.then_inc(S["bcu"], 1)
                            pe.wait_ge(S["scan"], i * EN + E + 1)
                            for c0, c1 in ((0, min(512, T[l])), (512, T[l])):
                                if c1 > c0:
                                    last = pe.matmul(pD[:, e % 2, c0:c1], sel[:, e, :], RD[:, s % 2, g, c0:c1],
                                                     start=True, stop=True)
                            last.then_inc(S["bcd"], 1)
                            pg = prev_group(s, g)
                            if pg is not None:
                                y_step(i, pg[0], pg[1], ITEMS[pg[0]][1], k_slots(ITEMS[pg[0]][1], spread(pg[1]))[e])
                            if g == 0 and e in (8, 10) and (e - 8) // 2 < len(halves(l)):
                                bank_free(i, ("c", s, (e - 8) // 2))
                                project(wc, l, a, *halves(l)[(e - 8) // 2])
                            if s > 0 and g == 0 and e >= 12:
                                for b in range(2):
                                    fin_step(i, s - 1, 0, e - 12, b)
                            if s > 0 and g == 1 and e in (2, 3):
                                for qb in range(4):
                                    fin_step(i, s - 1, 1, 2 * (e - 2) + qb // 2, qb % 2)
                            hn = halves(nl)
                            j = EG * (g - 2) + e
                            if j in (4, 6) and (j - 4) // 2 < len(hn):
                                h = (j - 4) // 2
                                if h == 0:
                                    if nl == 0:
                                        pe.wait_ge(S["xload"], 16 * (2 * i + (2 if n == 1 else 3)))
                                    else:
                                        pe.wait_ge(S["fin"], i * NI + n)
                                bank_free(i, ("z", n, h))
                                project(wr, nl, na, *hn[h])
                            if j in (14, 16) and (j - 14) // 2 < len(hn):
                                h = (j - 14) // 2
                                bank_free(i, ("b", n, h))
                                project(wb, nl, na, *hn[h])
                s = NI - 1
                for todo in k_slots(ITEMS[s][1], 12):
                    y_step(i, s, NG - 1, ITEMS[s][1], todo)
                for h in range(2):
                    for q in range(4):
                        for b in range(2):
                            fin_step(i, s, h, q, b)

        @block.scalar
        def _(act):
            def softplus(l, prep):
                act.wait_ge(S["zneg"], prep)
                act.activation(ss[:, 0:T[l]], ss[:, 0:T[l]], ACT.Exp).then_inc(S["sp1"], 1)
                act.wait_ge(S["sp1"], prep)
                act.activation(ss[:, 0:T[l]], ss[:, 0:T[l]], ACT.Ln, bias=1.0).then_inc(S["sp"], 1)

            def cast(l, part, src_done, counter, prep):
                for k, (dst, src) in enumerate(((dp, ss), (up, zz))):
                    act.wait_ge(S[src_done], 2 * prep - 1 + k)
                    if part == 0 and not isinstance(prep, int):
                        act.wait_ge(S["rdl" if k == 0 else "rul"], (prep - 1) * 16 * NSPLIT)
                    act.activation(dst[:, part, 0:T[l]], src[:, 0:T[l]], ACT.Copy).then_inc(S[counter], 1)

            def b_half(par, c0, c1, full_count):
                act.wait_ge(S["yfull"], full_count)
                act.activation(Bs[:, par, c0:c1], pY[:, 0:c1 - c0], ACT.Copy).then_inc(S["bev"], 1)

            def o_evac(i, s, g, j):
                l = ITEMS[s][1]
                k0, k1 = pieces(l)[j]
                act.wait_ge(S["ymm"], i * ON + ocount(s, g) + j + 1)
                if g == 0 and j == 0 and s > 0:
                    act.wait_ge(S["yfull"], i * YN + yb[("fin", s - 1, 1)] + 2 * ZPRE + 1)
                act.activation(osb[:, g, 2 * Q * k0:2 * Q * k1], pO[:, 0:2 * Q * (k1 - k0)], ACT.Copy)\
                    .then_inc(S["oev"], 1)

            def c_half(i, s, h, c0, c1):
                l = ITEMS[s][1]
                act.wait_ge(S["yfull"], i * YN + yb[("c", s, h)] + 2 * ZPRE + 1)
                cv = Cb[:, 0:2 * Q * TQ[l]].rearrange("p (k q b) -> p b q k", q=Q, b=2)
                tq = TQ[l]
                last = None
                runs = []
                q0, q1 = -(-c0 // tq), c1 // tq
                if c0 < q0 * tq:
                    runs.append((c0, q0 * tq))
                if q1 > q0:
                    runs.append((q0 * tq, q1 * tq))
                if q1 * tq < c1:
                    runs.append((q1 * tq, c1))
                for b in range(2):
                    for r0, r1 in runs:
                        pp = slice(64 * b, 64 * b + 64)
                        if (r1 - r0) > tq or (r1 - r0 == tq and r0 % tq == 0):
                            dst = cv[pp, b, r0 // tq:r1 // tq, :]
                            src = pY[pp, r0 - c0:r1 - c0].rearrange("p (q k) -> p q k", k=tq)
                        else:
                            q = r0 // tq
                            dst = cv[pp, b, q, r0 - q * tq:r1 - q * tq]
                            src = pY[pp, r0 - c0:r1 - c0]
                        last = act.activation(dst, src, ACT.Copy)
                last.then_inc(S["cev"], 1)

            act.wait_ge(S["hout"], 16)
            act.activation(sel[:].rearrange("k e m -> k (e m)"), hst[0:96, 0, 0:EG * P], ACT.Copy).then_inc(S["selc"], 1)
            act.preload_act_table_set("natural_log_exp_and_others")
            act.wait_ge(S["const"], 16 * (len(CONSTS) - 1))
            act.wait_ge(S["mset"], 1)
            act.activation(A[:], A[:], ACT.Exp).then_inc(S["aexp"], 1)
            act.wait_ge(S["aexp"], 1)
            act.activation(A[:], A[:], ACT.Copy, scale=-1.0).then_inc(S["aexp"], 1)
            act.wait_ge(S["aexp"], 2)
            act.activation(hd[:], hd[:], ACT.Copy, scale=0.5).then_inc(S["aexp"], 1)
            act.activation(ub[0:1, 0, 0:1], bd[0:1, 0:1], ACT.Copy).then_inc(S["ucopy"], 1)
            act.wait_ge(S["ucopy"], 1)
            act.wait_ge(S["aexp"], 3)

            def evac_z(l, c0, c1, full_count, prep):
                if prep is not None:
                    act.wait_ge(S["part"], 2 * (prep - 1))
                act.wait_ge(S["yfull"], full_count)
                act.activation(zz[:, c0:c1], pY[:, 0:c1 - c0], ACT.Identity, scale=wdt[:, l:l + 1],
                               bias=bd[:, l:l + 1]).then_inc(S["zev"], 1)

            for u, (c0, c1) in enumerate(halves(0)):
                evac_z(0, c0, c1, u + 1, None)
            softplus(0, 1)
            cast(0, 0, "dlt", "cast1", 1)
            cast(0, 1, "res1", "cast2", 1)
            for u, (c0, c1) in enumerate(halves(0)):
                b_half(0, c0, c1, ZPRE + u + 1)

            with act.Fori(0, HALF) as i:
                for s, (a, l) in enumerate(ITEMS):
                    n = (s + 1) % NI
                    nl = ITEMS[n][1]
                    for g in range(NG):
                        for e in range(EG):
                            E = D * s + EG * g + e
                            act.wait_ge(S["bcu"], i * EN + E + 1)
                            act.wait_ge(S["dbx"], i * EN + E + 1)
                            act.activation(ub[:, e % 2, 0:T[l]], pU[:, 0:T[l]], ACT.Copy).then_inc(S["ucopy"], 1)
                            act.wait_ge(S["bcd"], i * EN + E + 1)
                            act.activation(pD[:, e % 2, 0:T[l]], pD[:, e % 2, 0:T[l]], ACT.Exp,
                                           scale=A[:, l, EG * g + e:EG * g + e + 1]).then_inc(S["decay"], 1)
                            pg = prev_group(s, g)
                            if pg is not None:
                                for j, at in evac_slots(ITEMS[pg[0]][1], spread(pg[1])).items():
                                    if at == e - 1:
                                        o_evac(i, pg[0], pg[1], j)
                            if g == 0 and e in (9, 11) and (e - 9) // 2 < len(halves(l)):
                                c_half(i, s, (e - 9) // 2, *halves(l)[(e - 9) // 2])
                            hn = halves(nl)
                            j = EG * (g - 2) + e
                            prep = i * NI + s + 2
                            if j in (5, 7) and (j - 5) // 2 < len(hn):
                                h = (j - 5) // 2
                                evac_z(nl, *hn[h], i * YN + yb[("z", n, h)] + 2 * ZPRE + 1, prep)
                            if j == 9:
                                softplus(nl, prep)
                            if j == 11:
                                cast(nl, 0, "dlt", "cast1", prep)
                            if j == 13:
                                cast(nl, 1, "res1", "cast2", prep)
                            if j in (15, 17) and (j - 15) // 2 < len(hn):
                                h = (j - 15) // 2
                                b_half(n % 2, *hn[h], i * YN + yb[("b", n, h)] + 2 * ZPRE + 1)
                s = NI - 1
                for j in range(len(pieces(ITEMS[s][1]))):
                    o_evac(i, s, NG - 1, j)

        @block.gpsimd
        def _(pool):
            def residual(l, prep):
                pool.wait_ge(S["dlt"], 2 * prep)
                for k, (src, p) in enumerate(((ss, dp), (zz, up))):
                    pool.wait_ge(S["cast1"], 2 * prep - 1 + k)
                    pool.tensor_tensor(src[:, 0:T[l]], src[:, 0:T[l]], p[:, 0, 0:T[l]], ALU.subtract)\
                        .then_inc(S["res1"], 1)

            def third(l, prep):
                for k, (src, p) in enumerate(((ss, dp), (zz, up))):
                    pool.wait_ge(S["cast2"], 2 * prep - 1 + k)
                    pool.wait_ge(S["res1"], 2 * prep - 1 + k)
                    pool.tensor_tensor(p[:, 2, 0:T[l]], src[:, 0:T[l]], p[:, 1, 0:T[l]], ALU.subtract)\
                        .then_inc(S["part"], 1)

            pool.memset(db[:, 0, :], 0.0).then_inc(S["dbx"], 1)
            pool.memset(db[:, 1, :], 0.0).then_inc(S["dbx"], 1)
            pool.wait_ge(S["dbx"], 2)
            residual(0, 1)
            third(0, 1)
            with pool.Fori(0, HALF) as i:
                for s, (a, l) in enumerate(ITEMS):
                    nl = ITEMS[(s + 1) % NI][1]
                    for g in range(NG):
                        for e in range(EG):
                            E = D * s + EG * g + e
                            if g == 0 and e == 0:
                                pool.wait_ge(S["bev"], i * ZN + zcount(s + 1))
                            pool.wait_ge(S["ucopy"], i * EN + E + 2)
                            pool.wait_ge(S["scan"], i * EN + E + 1)
                            pool.tensor_tensor(db[:, e % 2, 0:T[l]], ub[:, e % 2, 0:T[l]], Bs[:, s % 2, 0:T[l]],
                                               ALU.mult).then_inc(S["dbx"], 1)
                            j = EG * (g - 2) + e
                            if j == 12:
                                residual(nl, i * NI + s + 2)
                            if j == 14:
                                third(nl, i * NI + s + 2)

        @block.vector
        def _(v):
            def negabs(l, zdone, prep):
                v.wait_ge(S["zev"], zdone)
                v.scalar_tensor_tensor(ss[:, 0:T[l]], zz[:, 0:T[l]], -1.0, zz[:, 0:T[l]], ALU.mult, ALU.min)\
                    .then_inc(S["zneg"], 1)

            def delta_u(l, a, prep):
                v.wait_ge(S["sp"], prep)
                v.scalar_tensor_tensor(ss[:, 0:T[l]], zz[:, 0:T[l]], 0.0, ss[:, 0:T[l]], ALU.max, ALU.add)\
                    .then_inc(S["dlt"], 1)
                v.wait_ge(S["dlt"], 2 * prep - 1)
                v.tensor_tensor(zz[:, 0:T[l]], ss[:, 0:T[l]], xs[l][:, a, :], ALU.mult).then_inc(S["dlt"], 1)

            def fin(i, s, h):
                a, l = ITEMS[s]
                c0, c1 = 4 * h * TQ[l], min(4 * (h + 1) * TQ[l], T[l])
                v.wait_ge(S["yfull"], i * YN + yb[("fin", s, h)] + 2 * ZPRE + 1)
                v.scalar_tensor_tensor(xf[:, c0:c1], xs[l][:, a, c0:c1], hd[:, l:l + 1], pY[:, 0:c1 - c0],
                                       ALU.mult, ALU.add).then_inc(S["fin1"], 1)
                if h == 1:
                    v.wait_ge(S["fin1"], 2 * (i * NI + s + 1) + 1)
                    if l < 2:
                        m = T[l + 1]
                        xv = xf[:, 0:2 * m].rearrange("p (t two) -> p two t", two=2)
                        if l == 1:
                            v.wait_ge(S["hout"], 16 * (2 * i + 1))
                        v.tensor_tensor(xs[l + 1][:, a, :], xv[:, 0, :], xv[:, 1, :], ALU.add).then_inc(S["fin"], 1)
                    else:
                        v.tensor_scalar(xs[2][:, a, :], xf[:, 0:T[2]], 2.0, None, ALU.mult).then_inc(S["fin"], 1)

            v.wait_ge(S["selc"], 1)
            v.memset(hst[:, 0, :], 0.0).then_inc(S["scan"], 1)
            v.memset(hst[:, 1, :], 0.0).then_inc(S["scan"], 1)
            v.memset(Cb[:], 0.0).then_inc(S["mset"], 1)
            v.memset(xf[:, 0:1], 0.0).then_inc(S["fin"], 1)
            v.memset(xf[:, 1:2], 0.0).then_inc(S["fin1"], 1)
            v.wait_ge(S["scan"], 2)
            v.wait_ge(S["mset"], 1)
            negabs(0, len(halves(0)), 1)
            v.wait_ge(S["xload"], 16)
            delta_u(0, 0, 1)
            v.wait_ge(S["aexp"], 3)
            with v.Fori(0, HALF) as i:
                for s, (a, l) in enumerate(ITEMS):
                    n = (s + 1) % NI
                    na, nl = ITEMS[n]
                    TP = Q * TQ[l]
                    for g in range(NG):
                        for e in range(EG):
                            E = D * s + EG * g + e
                            if e == 0:
                                m = ocount(s, g) - len(pieces(l)) if g > 0 else (ocount(s, 0) - len(pieces(ITEMS[s - 1][1])) if s > 0 else 0)
                                if m > 0:
                                    v.wait_ge(S["ymm"], i * ON + m)
                            v.wait_ge(S["decay"], i * EN + E + 1)
                            v.wait_ge(S["dbx"], i * EN + E + 3)
                            v.tensor_tensor_scan(hst[:, g % 2, e * TP:e * TP + T[l]], pD[:, e % 2, 0:T[l]],
                                                 db[:, e % 2, 0:T[l]], 0.0, ALU.mult, ALU.add).then_inc(S["scan"], 1)
                            if s > 0 and g == 1 and e == 1:
                                fin(i, s - 1, 0)
                            if s > 0 and g == 1 and e == 5:
                                fin(i, s - 1, 1)
                            j = EG * (g - 2) + e
                            if j == 8:
                                negabs(nl, i * ZN + zdone(n, len(halves(nl)) - 1), i * NI + s + 2)
                            if j == 10:
                                delta_u(nl, na, i * NI + s + 2)
                for h in range(2):
                    fin(i, NI - 1, h)



TK = 192
CH = 16
TL = 96
NC = TK // CH
CT = TL // CH
GP = 2
NCOL = GP * TK
NT_ = GP * TK // TL
NU = 2 * NT_
STEPS = PAIRS // GP
TR = T[2]
DECAY = -0.6065306597126334
MIX = ("r", "w", "k", "v", "a", "g")
EXPERTS = 8
EJ = EXPERTS // 2


class Steps:

    def __init__(self, sem, names):
        self.sem, self.names, self.at, self.n = sem, names, {n: k + 1 for k, n in enumerate(names)}, len(names)

    def value(self, i, name):
        return i * self.n + self.at[name]


def mixer_phase(nc, ctx, W, hid, hall, x2all):
    sb = lambda n, s, d=F32: ctx.enter_context(nc.sbuf_tensor(n, s, d))
    sem = lambda n: ctx.enter_context(nc.semaphore(n))
    bank = [ctx.enter_context(nc.psum_tensor(f"bank{k}", [P, 512], F32)) for k in range(8)]
    F = lambda n: sb(n, [P, NCOL])

    const = {k: sb("c_" + k, list(W[k].shape), F32) for k in
             ("ones", "ones64", "ident", "wk", "ww", "wa", "wr_", "wv", "wg", "wbw", "wba", "wbg", "wo",
              "vec", "m_lt", "m_l", "m_ka", "m_kr", "m_br", "cm", "cmn", "eye6", "smask")}
    c = const
    VEC = {n: k for k, n in enumerate(("mix_r", "mix_w", "mix_k", "mix_v", "mix_a", "mix_g", "b_w", "b_a", "k_k",
                                       "k_a", "r_k", "gn_w", "gn_b"))}
    vec = lambda n: c["vec"][:, VEC[n]:VEC[n] + 1]
    cst = sb("cst", [P, 4])
    xc, sq, rs, dx, t1, t2, ha, aa = (F(n) for n in ("xc", "sq", "rs", "dx", "t1", "t2", "ha", "aa"))
    xp = sb("xp", [P, GP, TK + 1])
    xm = {m: F("xm_" + m) for m in MIX}
    kk, kp, bb, ww, cs, al, be, ka, rho, rk, vF, bon, gF = (
        F(n) for n in ("kk", "kp", "bb", "ww", "cs", "al", "be", "ka", "rho", "rk", "vF", "bon", "gF"))
    Pi, Pn, Pe = xm["w"], xm["a"], xm["k"]
    oF, oc = xm["r"], xm["v"]
    gh = sb("gh", [P, 2, NCOL])
    VN, bN, kN = (sb(n, [TL, NT_, P]) for n in ("VN", "bN", "kN"))
    Y = sb("Y", [TL, NT_, 2, P])
    mats = {n: sb("g_" + n, [TL, NU, TL]) for n in ("NT", "N", "KA", "KR", "BR", "N2T", "N2", "N4T", "N4", "N8T")}
    bX, vX, uX = (sb(n, [TL, NT_, 2, CT, D]) for n in ("bX", "vX", "uX"))
    GT, HP = (sb(n, [P, NT_, CT * D]) for n in ("GT", "HP"))
    M = sb("M", [P, NC, GP, D])

    s_const, s_h, s_set = sem("m_const"), sem("m_h"), sem("m_set")
    PE = Steps(sem("m_pe"), ["mean", "var", "k", "hw", "ha", "r", "vF", "vN", "hg0", "hg1", "w", "a", "g", "ss", "bsum",
                             "tA", "tB", "tK", "LT", "L", "KA", "KR", "BR", "LKV", "Y1a", "Y1b", "N2T", "N2", "Y2a",
                             "Y2b", "N4T", "N4", "Y3a", "Y3b", "N8T", "Y4a", "Y4b"]
               + ["GT%d" % k for k in range(NT_)] + ["HP%d" % k for k in range(NT_)] + ["RT"]
               + ["M%d" % k for k in range(2, NC)] + ["O", "omean", "ovar", "out", "mean2", "var2"])
    AC = Steps(sem("m_act"), ["lnv", "rstd", "ew", "hac", "vFc", "VN", "eg0", "eg1", "ew2", "ea", "lnk", "rk",
                              "gF", "Pi", "Pn", "Pe", "aN", "bN", "kN", "LKV", "N2T", "N2", "N4T", "N4", "N8T",
                              "oF", "lno", "rstdo", "lnv2", "rstd2"])
    DV = Steps(sem("m_dve"), ["xc", "sq", "x", "dx"] + ["mix_" + m for m in ("k", "w", "a", "r", "v", "g")]
               + ["w1", "w2", "w3", "s1", "s2", "s3", "a1", "a2", "g1", "g2", "kk", "kk2", "ssm", "kkn", "ka1", "kp", "b",
                  "cs", "ce", "al", "be", "ka", "rho", "rk", "bon", "NT", "N", "KA", "KR", "BR", "Y1a", "Y1b", "Y2a", "Y2b",
                  "Y3a", "Y3b", "Y4a", "Y4b", "uX"]
               + ["GT%d" % k for k in range(NT_)] + ["HP%d" % k for k in range(NT_)] + ["RT", "M1"]
               + ["M%d" % k for k in range(2, NC)]
               + ["oc", "osq", "on1", "on2", "on3", "on4", "hn", "xc2", "sq2", "x2"])
    PL = Steps(sem("m_pool"), ["bX", "vX"])

    class On:

        def __init__(self, eng, own, i):
            self.eng, self.own, self.i, self.k = eng, own, i, 0

        def need(self, steps, *names):
            last = max(names, key=lambda n: steps.at[n])
            self.eng.wait_ge(steps.sem, steps.value(self.i, last))

        def step(self, name, ins):
            assert self.own.names[self.k] == name, (self.own.names[self.k], name)
            self.k += 1
            ins.then_inc(self.own.sem, 1)

    def cols(i):
        return bass.ds(i * NCOL, NCOL)

    hflat = hall[:].rearrange("p a t -> p (a t)")
    xflat = x2all[:].rearrange("p a t -> p (a t)")
    pr = lambda t: t[:].rearrange("p (a t) -> p a t", t=TK)
    unit4 = lambda b: bank[b][0:TL, 0:4 * TL].rearrange("p (u t) -> p u t", t=TL)

    with nc.Block() as block:
        @block.sync
        def _(sp):
            for k in const:
                sp.dma_start(const[k][:], W[k]).then_inc(s_const, 16)
            sp.wait_ge(s_set, 4)
            for p in range(PAIRS):
                sp.dma_start(hall[:, p, 0:TR], hid[p, :, :]).then_inc(s_h, 16)

        @block.gpsimd
        def _(pool):
            pool.memset(hall[:], 0.0).then_inc(s_set, 1)
            pool.memset(cst[:, 0:1], 1e-5).then_inc(s_set, 1)
            pool.memset(cst[:, 1:2], D * 1e-5).then_inc(s_set, 1)
            pool.memset(cst[:, 2:3], 15 * 0.6931471805599453).then_inc(s_set, 1)
            pool.wait_ge(s_const, 16 * len(const))
            with pool.Fori(0, STEPS) as i:
                o = On(pool, PL, i)
                for name, src, dst in (("bX", bN, bX), ("vX", VN, vX)):
                    o.need(AC, "bN" if name == "bX" else "VN")
                    for k in range(NT_):
                        ins = pool.tensor_tensor(dst[:, k], src[:, k, :].rearrange("p (b f) -> p b f", b=2)
                                                 .unsqueeze(2).to_broadcast([TL, 2, CT, D]),
                                                 c["cm"][:].unsqueeze(1).unsqueeze(3).to_broadcast([TL, 2, CT, D]),
                                                 ALU.mult)
                    o.step(name, ins)

        @block.tensor
        def _(pe):
            pe.wait_ge(s_const, 16 * len(const))
            pe.wait_ge(s_h, 16 * PAIRS)
            with pe.Fori(0, STEPS) as i:
                o = On(pe, PE, i)
                mm = lambda out, l, r, a=True, z=True: pe.matmul(out, l, r, start=a, stop=z)
                full = lambda b: bank[b][:, 0:NCOL]
                pe.wait_ge(DV.sem, i * DV.n)
                o.step("mean", mm(full(0), c["ones64"][:], hflat[:, cols(i)]))
                o.need(DV, "sq")
                o.step("var", mm(full(1), c["ones64"][:], sq[:]))
                for name, b, w, m in (("k", 2, "wk", "k"), ("hw", 3, "ww", "w"), ("ha", 4, "wa", "a"),
                                      ("r", 5, "wr_", "r"), ("vF", 6, "wv", "v")):
                    o.need(DV, "mix_" + m)
                    o.step(name, mm(full(b), c[w][:], xm[m][:]))
                for k in range(NT_):
                    ins = mm(bank[7][0:TL, P * k:P * k + P], xm["v"][:, TL * k:TL * k + TL], c["wv"][:])
                o.step("vN", ins)
                o.need(DV, "mix_g")
                o.need(AC, "lnv")
                for b in range(2):
                    o.step("hg%d" % b, mm(full(b), c["wg"][64 * b:64 * b + 64, :], xm["g"][64 * b:64 * b + 64, :]))
                o.need(DV, "w3")
                o.step("w", mm(full(3), c["wbw"][:], t1[:]))
                o.need(AC, "hac")
                o.step("a", mm(full(4), c["wba"][:], ha[:]))
                o.need(DV, "g2")
                for b in range(2):
                    ins = mm(bank[0][64 * b:64 * b + 64, 0:NCOL], c["wbg"][:], gh[:, b, :])
                o.step("g", ins)
                o.need(DV, "kk2")
                o.step("ss", mm(full(1), c["ones"][:], sq[:]))
                o.need(DV, "rk")
                o.step("bsum", mm(full(5), c["ones"][:], rk[:]))
                for name, b, src, free in (("tA", 6, al, (AC, "vFc")), ("tB", 7, be, (AC, "VN")),
                                           ("tK", 2, ka, (DV, "kp"))):
                    o.need(*free)
                    for k in range(NT_):
                        ins = pe.transpose(bank[b][0:TL, P * k:P * k + P], src[:, TL * k:TL * k + TL], c["ident"][:])
                    o.step(name, ins)
                for name, (l, r), b0, free in (
                        ("LT", (be, al), 3, ((AC, "ew2"), (AC, "ea"))), ("L", (al, be), 0, ((AC, "gF"), (DV, "ssm"))),
                        ("KA", (ka, al), 3, ((DV, "NT"),)), ("KR", (ka, rho), 0, ((DV, "N"),)),
                        ("BR", (be, rho), 3, ((DV, "KA"),))):
                    for f in free:
                        o.need(*f)
                    for u in range(NU):
                        b, k = divmod(u, NT_)
                        sl = slice(64 * b, 64 * b + 64)
                        ins = mm(unit4(b0 + b)[:, k, :], l[sl, TL * k:TL * k + TL],
                                 r[sl, TL * k:TL * k + TL])
                    o.step(name, ins)
                o.need(DV, "KA", "bon")
                o.need(AC, "VN")
                for u in range(NU):
                    k, b = divmod(u, 2)
                    ins = mm(bank[5][0:TL, D * u:D * u + D], mats["KA"][:, NT_ * b + k, :], VN[:, k, 64 * b:64 * b + 64])
                o.step("LKV", ins)

                def apply(mat, tag):
                    for h, x in enumerate("ab"):
                        for u in range(4 * h, 4 * h + 4):
                            k, b = divmod(u, 2)
                            ins = mm(bank[6 + h][0:TL, P * (u % 4):P * (u % 4) + P], mats[mat][:, NT_ * b + k, :], Y[:, k, b, :])
                        o.step(tag + x, ins)

                def square(name, l, r, b0):
                    for u in range(NU):
                        ins = mm(unit4(b0 + u // 4)[:, u % 4, :], mats[l][:, u, :], mats[r][:, u, :])
                    o.step(name, ins)

                o.need(AC, "LKV", "aN", "bN")
                apply("NT", "Y1")
                o.need(DV, "BR")
                square("N2T", "N", "NT", 3)
                square("N2", "NT", "N", 0)
                o.need(AC, "N2")
                o.need(DV, "Y1b")
                apply("N2T", "Y2")
                square("N4T", "N2", "N2T", 3)
                square("N4", "N2T", "N2", 0)
                o.need(AC, "N4")
                o.need(DV, "Y2b")
                apply("N4T", "Y3")
                square("N8T", "N4", "N4T", 3)
                o.need(AC, "N8T")
                o.need(DV, "Y3b")
                apply("N8T", "Y4")
                o.need(DV, "Y4b")
                o.need(PL, "bX")
                for k in range(NT_):
                    for b in range(2):
                        ins = mm(bank[k][64 * b:64 * b + 64, 0:CT * D], Y[:, k, b, 0:D],
                                 bX[:, k, b].rearrange("p c f -> p (c f)"))
                    o.step("GT%d" % k, ins)
                o.need(DV, "uX")
                o.need(PL, "vX")
                for k in range(NT_):
                    for b in range(2):
                        out = bank[4 + k][64 * b:64 * b + 64, 0:CT * D]
                        mm(out, kN[:, k, 64 * b:64 * b + 64], vX[:, k, b].rearrange("p c f -> p (c f)"), True, False)
                        ins = mm(out, bN[:, k, 64 * b:64 * b + 64], uX[:, k, b].rearrange("p c f -> p (c f)"),
                                 False, True)
                    o.step("HP%d" % k, ins)
                o.need(DV, "GT0")
                for u in range(NU):
                    k, b = divmod(u, 2)
                    ins = mm(bank[0][64 * b:64 * b + 64, TL * k:TL * k + TL], Y[:, k, b, 0:D], mats["BR"][:, NT_ * b + k, :])
                o.step("RT", ins)
                o.need(DV, "HP3")
                for ci in range(1, NC - 1):
                    o.need(DV, "M%d" % ci)
                    half, cc = divmod(ci, CT)
                    mm(bank[1 + ci % 2][:, 0:GP * D], c["ident"][:],
                       HP[:].rearrange("p (a h) (c f) -> p a h c f", h=2, f=D)[:, :, half, cc, :], True, False)
                    for p in range(GP):
                        for b in range(2):
                            sl = slice(64 * b, 64 * b + 64)
                            ins = mm(bank[1 + ci % 2][sl, D * p:D * p + D], GT[sl, 2 * p + half, D * cc:D * cc + D],
                                     M[sl, ci, p, :], False, p == GP - 1)
                    o.step("M%d" % (ci + 1), ins)
                o.need(DV, "M%d" % (NC - 1))
                for u in range(NU):
                    k, b = divmod(u, 2)
                    sl = slice(64 * b, 64 * b + 64)
                    p, half = divmod(k, 2)
                    mm(bank[3][sl, TL * k:TL * k + TL], VN[:, k, sl], mats["KR"][:, NT_ * b + k, :], True, False)
                    chunks = [x for x in range(CT) if half or x]
                    mm(bank[3][sl, TL * k:TL * k + TL], Y[:, k, b, D:P], mats["BR"][:, NT_ * b + k, :], False, False)
                    for cc in chunks:
                        c0 = TL * k + CH * cc
                        ins = mm(bank[3][sl, c0:c0 + CH], M[sl, CT * half + cc, p, :], al[sl, c0:c0 + CH], False,
                                 cc == chunks[-1])
                o.step("O", ins)
                o.need(AC, "oF")
                o.step("omean", mm(full(4), c["ones64"][:], oF[:]))
                o.need(DV, "osq")
                o.step("ovar", mm(full(5), c["ones64"][:], sq[:]))
                o.need(DV, "on4")
                o.step("out", mm(full(6), c["wo"][:], t1[:]))
                o.need(DV, "hn")
                o.step("mean2", mm(full(7), c["ones64"][:], hflat[:, cols(i)]))
                o.need(DV, "sq2")
                o.step("var2", mm(full(0), c["ones64"][:], sq[:]))

        @block.scalar
        def _(act):
            A = lambda out, in_, f, **k: act.activation(out, in_, f, **k)
            act.preload_act_table_set("natural_log_exp_and_others")
            act.wait_ge(s_const, 16 * len(const))
            act.wait_ge(s_set, 4)
            A(c["vec"][:, 6:8], c["vec"][:, 6:8], ACT.Copy, scale=-1.0).then_inc(s_set, 1)
            act.wait_ge(s_set, 5)
            with act.Fori(0, STEPS) as i:
                o = On(act, AC, i)
                full = lambda b: bank[b][:, 0:NCOL]

                def rstd(src, eps, pe_step, a, b):
                    o.need(PE, pe_step)
                    o.step(a, A(rs[:], full(src), ACT.Ln, bias=eps))
                    o.need(AC, a)
                    o.step(b, A(rs[:], rs[:], ACT.Exp, scale=-0.5))

                rstd(1, cst[:, 0:1], "var", "lnv", "rstd")
                o.need(PE, "hw")
                o.step("ew", A(t1[:], full(3), ACT.Exp, scale=2.0))
                o.need(PE, "ha")
                o.step("hac", A(ha[:], full(4), ACT.Copy))
                o.need(PE, "vF")
                o.step("vFc", A(vF[:], full(6), ACT.Copy))
                o.need(PE, "vN")
                o.step("VN", A(VN[:].rearrange("p k f -> p (k f)"), bank[7][0:TL, :], ACT.Copy))
                for b in range(2):
                    o.need(PE, "hg%d" % b)
                    o.step("eg%d" % b, A(gh[:, b, :], full(b), ACT.Exp, scale=-1.0))
                o.need(PE, "w")
                o.step("ew2", A(t2[:], full(3), ACT.Exp, scale=-1.0, bias=vec("b_w")))
                o.need(PE, "a")
                o.step("ea", A(aa[:], full(4), ACT.Exp, scale=-1.0, bias=vec("b_a")))
                o.need(DV, "ssm")
                o.step("lnk", A(rs[:], sq[:], ACT.Ln, scale=float(2 ** 30)))
                o.need(AC, "lnk")
                o.step("rk", A(rs[:], rs[:], ACT.Exp, scale=-0.5, bias=cst[:, 2:3]))
                o.need(PE, "g")
                o.step("gF", A(gF[:], full(0), ACT.Copy))
                o.need(DV, "cs")
                o.step("Pi", A(Pi[:], cs[:], ACT.Exp))
                o.step("Pn", A(Pn[:], cs[:], ACT.Exp, scale=-1.0))
                o.need(DV, "ce")
                o.step("Pe", A(Pe[:], ww[:], ACT.Exp))
                o.need(PE, "tA")
                o.step("aN", A(Y[:, :, :, 0:D], bank[6][0:TL, :].rearrange("p (k b f) -> p k b f", b=2, f=D), ACT.Copy))
                o.need(PE, "tB")
                o.step("bN", A(bN[:].rearrange("p k f -> p (k f)"), bank[7][0:TL, :], ACT.Copy))
                o.need(PE, "tK")
                o.step("kN", A(kN[:].rearrange("p k f -> p (k f)"), bank[2][0:TL, :], ACT.Copy))
                o.need(PE, "LKV")
                o.step("LKV", A(Y[:, :, :, D:P], bank[5][0:TL, :].rearrange("p (k b f) -> p k b f", b=2, f=D), ACT.Copy))
                for name, b0 in (("N2T", 3), ("N2", 0), ("N4T", 3), ("N4", 0), ("N8T", 3)):
                    o.need(PE, name)
                    for h in range(2):
                        ins = A(mats[name][:, 4 * h:4 * h + 4, :], unit4(b0 + h), ACT.Copy)
                    o.step(name, ins)
                o.need(PE, "O")
                o.step("oF", A(oF[:], full(3), ACT.Copy))
                rstd(5, cst[:, 1:2], "ovar", "lno", "rstdo")
                rstd(0, cst[:, 0:1], "var2", "lnv2", "rstd2")

        @block.vector
        def _(v):
            v.wait_ge(s_const, 16 * len(const))
            v.wait_ge(s_h, 16 * PAIRS)
            v.wait_ge(s_set, 5)
            v.memset(xp[:], 0.0).then_inc(s_set, 1)
            v.wait_ge(s_set, 6)
            with v.Fori(0, STEPS) as i:
                o = On(v, DV, i)
                tt, st, ts = v.tensor_tensor, v.scalar_tensor_tensor, v.tensor_scalar
                full = lambda b: bank[b][:, 0:NCOL]

                def own(*names):
                    o.need(DV, *names)

                def layer_center(b, pe_step, a, s):
                    o.need(PE, pe_step)
                    o.step(a, tt(xc[:], hflat[:, cols(i)], full(b), ALU.subtract))
                    own(a)
                    o.step(s, tt(sq[:], xc[:], xc[:], ALU.mult))

                layer_center(0, "mean", "xc", "sq")
                o.need(AC, "rstd")
                o.step("x", tt(xp[:, :, 1:TK + 1], pr(xc), pr(rs), ALU.mult))
                own("x")
                o.step("dx", tt(pr(dx), xp[:, :, 0:TK], xp[:, :, 1:TK + 1], ALU.subtract))
                own("dx")
                for m in ("k", "w", "a", "r", "v", "g"):
                    o.step("mix_" + m, st(pr(xm[m]), pr(dx), vec("mix_" + m), xp[:, :, 1:TK + 1], ALU.mult, ALU.add))

                def one_over_one_plus(t, a, b):
                    o.step(a, ts(t, t, 1.0, None, ALU.add))
                    own(a)
                    o.step(b, v.reciprocal(t, t))

                o.need(AC, "ew")
                one_over_one_plus(t1[:], "w1", "w2")
                own("w2")
                o.step("w3", ts(t1[:], t1[:], -2.0, 1.0, ALU.mult, ALU.add))
                o.need(AC, "ew2")
                one_over_one_plus(t2[:], "s1", "s2")
                own("s2")
                o.step("s3", ts(ww[:], t2[:], DECAY, None, ALU.mult))
                o.need(AC, "ea")
                one_over_one_plus(aa[:], "a1", "a2")
                o.need(AC, "eg1")
                one_over_one_plus(gh[:], "g1", "g2")
                o.need(PE, "k")
                o.step("kk", ts(kk[:], full(2), vec("k_k"), None, ALU.mult))
                own("kk")
                o.step("kk2", tt(sq[:], kk[:], kk[:], ALU.mult))
                o.need(PE, "ss")
                o.step("ssm", ts(sq[:], full(1), 1e-24, None, ALU.max))
                o.need(AC, "rk")
                o.step("kkn", tt(kk[:], kk[:], rs[:], ALU.mult))
                own("a2")
                o.step("ka1", ts(t2[:], aa[:], 1.0, vec("k_a"), ALU.subtract, ALU.mult))
                own("ka1")
                o.step("kp", st(kp[:], t2[:], 1.0, full(2), ALU.add, ALU.mult))
                own("kkn")
                o.step("b", tt(bb[:], kk[:], aa[:], ALU.mult))
                own("s3")
                o.step("cs", v.tensor_tensor_scan(cs[:], c["smask"][:], ww[:], 0.0, ALU.mult, ALU.add))
                own("cs")
                o.step("ce", tt(ww[:], cs[:], ww[:], ALU.subtract))
                o.need(AC, "Pe")
                o.step("al", tt(al[:], kk[:], Pe[:], ALU.mult))
                own("b")
                o.step("be", tt(be[:], bb[:], Pn[:], ALU.mult))
                o.step("ka", tt(ka[:], kp[:], Pn[:], ALU.mult))
                o.need(PE, "r")
                o.step("rho", tt(rho[:], full(5), Pi[:], ALU.mult))
                o.step("rk", st(rk[:], full(5), vec("r_k"), kp[:], ALU.mult, ALU.mult))
                o.need(PE, "bsum")
                o.need(AC, "vFc")
                o.step("bon", tt(bon[:], full(5), vF[:], ALU.mult))
                for name, pe_step, b0, mask in (("NT", "LT", 3, "m_lt"), ("N", "L", 0, "m_l"), ("KA", "KA", 3, "m_ka"),
                                                ("KR", "KR", 0, "m_kr"), ("BR", "BR", 3, "m_br")):
                    o.need(PE, pe_step)
                    for h in range(2):
                        ins = tt(mats[name][:, 4 * h:4 * h + 4, :], unit4(b0 + h),
                                 c[mask][:].unsqueeze(1).to_broadcast([TL, 4, TL]), ALU.mult)
                    o.step(name, ins)
                o.need(AC, "LKV")
                for n in range(1, 5):
                    for h, x in enumerate("ab"):
                        o.need(PE, "Y%d%s" % (n, x))
                        if n > 1:
                            own("Y%d%s" % (n - 1, x))
                        yv = Y[:, 2 * h:2 * h + 2].rearrange("p k b f -> p (k b f)")
                        o.step("Y%d%s" % (n, x), tt(yv, yv, bank[6 + h][0:TL, :], ALU.add))
                own("Y4b")
                for k in range(NT_):
                    ins = tt(uX[:, k], Y[:, k, :, D:P].unsqueeze(2).to_broadcast([TL, 2, CT, D]),
                             c["cmn"][:].unsqueeze(1).unsqueeze(3).to_broadcast([TL, 2, CT, D]), ALU.mult)
                o.step("uX", ins)
                for k in range(NT_):
                    o.need(PE, "GT%d" % k)
                    o.step("GT%d" % k, st(GT[:, k, :], full(k), -1.0, c["eye6"][:], ALU.mult, ALU.add))
                pend = pr(Pi)[:, :, CH - 1:TK:CH]
                for k in range(NT_):
                    o.need(PE, "HP%d" % k)
                    o.step("HP%d" % k, v.tensor_copy(HP[:, k, :], full(4 + k)))
                o.need(PE, "RT")
                o.step("RT", tt(al[:], rho[:], full(0), ALU.add))
                own("HP3")
                hv = HP[:].rearrange("p (a h) (c f) -> p a h c f", h=2, f=D)
                o.step("M1", tt(M[:, 1], hv[:, :, 0, 0, :], pend[:, :, 0:1].to_broadcast([P, GP, D]), ALU.mult))
                for ci in range(2, NC):
                    o.need(PE, "M%d" % ci)
                    o.step("M%d" % ci, tt(M[:, ci], bank[1 + (ci - 1) % 2][:, 0:GP * D]
                                          .rearrange("p (a f) -> p a f", f=D),
                                          pend[:, :, ci - 1:ci].to_broadcast([P, GP, D]), ALU.mult))
                o.need(PE, "omean")
                o.step("oc", tt(oc[:], oF[:], full(4), ALU.subtract))
                own("oc")
                o.step("osq", tt(sq[:], oc[:], oc[:], ALU.mult))
                o.need(AC, "rstdo")
                o.step("on1", tt(t1[:], oc[:], rs[:], ALU.mult))
                own("on1")
                o.step("on2", ts(t1[:], t1[:], vec("gn_w"), vec("gn_b"), ALU.mult, ALU.add))
                own("on2")
                o.step("on3", tt(t1[:], t1[:], bon[:], ALU.add))
                own("on3")
                o.step("on4", tt(t1[:], t1[:], gF[:], ALU.mult))
                o.need(PE, "out")
                o.step("hn", tt(hflat[:, cols(i)], hflat[:, cols(i)], full(6), ALU.add))
                own("hn")
                layer_center(7, "mean2", "xc2", "sq2")
                o.need(AC, "rstd2")
                o.step("x2", tt(xflat[:, cols(i)], xc[:], rs[:], ALU.mult))


def expert_phase(nc, ctx, W, hall, x2all, out):
    sb = lambda n, s, d=F32: ctx.enter_context(nc.sbuf_tensor(n, s, d))
    sem = lambda n: ctx.enter_context(nc.semaphore(n))
    bank = [ctx.enter_context(nc.psum_tensor(f"fbank{k}", [P, 512], F32)) for k in range(8)]
    names = ("fw1", "fw2", "fwo", "fwr", "fbr", "fbo", "fsel", "fbn", "ident")
    c = {k: sb("f_" + k, list(W[k].shape), F32) for k in names}
    eps = sb("f_eps", [P, 1])
    sc = sb("f_sc", [P, 2, EJ])
    bi = sb("f_bi", [P, 2, EJ])
    fs = sb("f_sum", [P, TK])
    lg, ex = (sb(n, [TL, 2, EXPERTS]) for n in ("f_lg", "f_ex"))
    mx, su = (sb(n, [TL, 2, 1]) for n in ("f_mx", "f_su"))
    wT = sb("f_wT", [EXPERTS, TK])
    wb = sb("f_wb", [P, EJ, TK])
    bw = sb("f_bw", [P, TK])
    H1 = sb("f_h1", [P, 4, NCOL])
    H2 = sb("f_h2", [P, 4, NCOL])
    fo = sb("f_out", [P, 2, NCOL])
    s = {n: sem("f_" + n) for n in ("const", "eps", "bn", "rt", "pe1", "act1", "mm1", "act_1", "mm2", "act_2", "wgt",
                                    "mm3", "res", "store")}
    hflat = hall[:].rearrange("p a t -> p (a t)")
    xflat = x2all[:].rearrange("p a t -> p (a t)")
    BNA = lambda what: c["fbn"][:, :, what, :]
    M2 = (4, 5, 7)
    BN = lambda layer, what: c["fbn"][:, layer, what, :]
    U = 2 * EJ

    with nc.Block() as block:
        @block.sync
        def _(sp):
            for k in names:
                sp.dma_start(c[k][:], W[k]).then_inc(s["const"], 16)
            sp.dma_start(fo[:, 1, 1:P + 1], W["ident"]).then_inc(s["store"], 16)
            with sp.Fori(0, STEPS) as i:
                sp.wait_ge(s["res"], 2 * i + 3)
                sp.wait_ge(s["const"], 16 * len(names))
                for p in range(GP):
                    src = i * GP + p
                    sp.dma_start(out[bass.ds(src, 1), :, :].rearrange("o p t -> p (o t)"),
                                 fo[:, 0, TK * p:TK * p + TR]).then_inc(s["store"], 16)
            sp.wait_ge(s["store"], 16 * (PAIRS + 1))

        @block.scalar
        def _(act):
            act.preload_act_table_set("natural_log_exp_and_others")
            act.wait_ge(s["const"], 16 * len(names))
            act.wait_ge(s["eps"], 1)
            for l in range(2):
                act.activation(sc[:, l], BN(l, 4), ACT.Ln, bias=eps[:, 0:1]).then_inc(s["act1"], 1)
            act.wait_ge(s["act1"], 2)
            act.activation(sc[:], sc[:], ACT.Exp, scale=-0.5).then_inc(s["act1"], 1)
            act.wait_ge(s["rt"], 4)
            act.activation(ex[:], lg[:], ACT.Exp).then_inc(s["act1"], 1)
            act.wait_ge(s["bn"], 4)
            with act.Fori(0, STEPS) as i:
                act.wait_ge(s["res"], 2 * i + 1)
                for u in range(U + 2):
                    if u < U:
                        act.wait_ge(s["mm1"], i * U + u + 1)
                        if u >= 4:
                            act.wait_ge(s["mm2"], i * U + u - 3)
                        act.activation(H1[:, u % 4, :], bank[u % 4][:, 0:NCOL], ACT.Relu,
                                       scale=sc[:, 0, u // 2:u // 2 + 1], bias=bi[:, 0, u // 2:u // 2 + 1])\
                            .then_inc(s["act_1"], 1)
                    if u >= 2:
                        w = u - 2
                        act.wait_ge(s["mm2"], i * U + w + 1)
                        if w >= 4:
                            act.wait_ge(s["mm3"], i * U + w - 3)
                        act.activation(H2[:, w % 4, :], bank[M2[w % 3]][:, 0:NCOL], ACT.Relu,
                                       scale=sc[:, 1, w // 2:w // 2 + 1], bias=bi[:, 1, w // 2:w // 2 + 1])\
                            .then_inc(s["act_2"], 1)

        @block.tensor
        def _(pe):
            mm = lambda out, l, r, a=True, z=True: pe.matmul(out, l, r, start=a, stop=z)
            pe.wait_ge(s["const"], 16 * len(names))
            pe.wait_ge(s["rt"], 1)
            for h in range(2):
                ins = mm(bank[7][0:TL, 8 * h:8 * h + 8], fs[:, TL * h:TL * h + TL], c["fwr"][:])
            ins.then_inc(s["pe1"], 1)
            pe.wait_ge(s["rt"], 7)
            for h in range(2):
                ins = pe.transpose(bank[6][0:EXPERTS, TL * h:TL * h + TL], ex[:, h, :], c["ident"][0:TL, 0:TL])
            ins.then_inc(s["pe1"], 1)
            pe.wait_ge(s["rt"], 8)
            for j in range(EJ):
                ins = mm(bank[j][:, 0:TK], c["fsel"][:, j, :], wT[:])
            ins.then_inc(s["pe1"], 1)
            mm(bank[5][:, 0:TK], c["fbo"][:], wT[:]).then_inc(s["pe1"], 1)
            pe.wait_ge(s["rt"], 10)
            with pe.Fori(0, STEPS) as i:
                for u in range(U + 3):
                    if u < U:
                        j, b = divmod(u, 2)
                        if u >= 4:
                            pe.wait_ge(s["act_1"], i * U + u - 3)
                        mm(bank[u % 4][:, 0:NCOL], c["fw1"][:, b, j, :], xflat[:, bass.ds(i * NCOL, NCOL)])\
                            .then_inc(s["mm1"], 1)
                    if 1 <= u <= U:
                        w = u - 1
                        pe.wait_ge(s["act_1"], i * U + w + 1)
                        if w >= 3:
                            pe.wait_ge(s["act_2"], i * U + w - 2)
                        mm(bank[M2[w % 3]][:, 0:NCOL], c["fw2"][:, w // 2, :], H1[:, w % 4, :]).then_inc(s["mm2"], 1)
                    if u >= 3:
                        w = u - 3
                        j, b = divmod(w, 2)
                        if w == 0:
                            pe.wait_ge(s["res"], 2 * i + 1)
                        pe.wait_ge(s["wgt"], i * U + w + 1)
                        mm(bank[6][64 * b:64 * b + 64, 0:NCOL], c["fwo"][:, j, :], H2[:, w % 4, :], j == 0,
                           j == EJ - 1).then_inc(s["mm3"], 1)

        @block.vector
        def _(v):
            tt = v.tensor_tensor
            v.memset(eps[:], 1e-3).then_inc(s["eps"], 1)
            v.memset(fo[:, 1, 0:1], 0.0).then_inc(s["res"], 1)
            v.tensor_reduce(fs[:], x2all[:].rearrange("p a t -> p t a"), axis=AX_X, op=ALU.add).then_inc(s["rt"], 1)
            v.wait_ge(s["const"], 16 * len(names))
            v.wait_ge(s["pe1"], 1)
            v.scalar_tensor_tensor(lg[:], bank[7][0:TL, 0:16].rearrange("p (h e) -> p h e", h=2), 1.0 / (2 * PAIRS),
                                   c["fbr"][:], ALU.mult, ALU.add).then_inc(s["rt"], 1)
            v.wait_ge(s["rt"], 2)
            v.tensor_reduce(mx[:], lg[:], axis=AX_X, op=ALU.max).then_inc(s["rt"], 1)
            v.wait_ge(s["rt"], 3)
            tt(lg[:], lg[:], mx[:].to_broadcast([TL, 2, EXPERTS]), ALU.subtract).then_inc(s["rt"], 1)
            v.wait_ge(s["act1"], 3)
            tt(sc[:], sc[:], BNA(1), ALU.mult).then_inc(s["bn"], 1)
            tt(bi[:], BNA(0), BNA(3), ALU.subtract).then_inc(s["bn"], 1)
            v.wait_ge(s["bn"], 2)
            tt(bi[:], bi[:], sc[:], ALU.mult).then_inc(s["bn"], 1)
            v.wait_ge(s["bn"], 3)
            tt(bi[:], bi[:], BNA(2), ALU.add).then_inc(s["bn"], 1)
            v.wait_ge(s["act1"], 4)
            v.tensor_reduce(su[:], ex[:], axis=AX_X, op=ALU.add).then_inc(s["rt"], 1)
            v.wait_ge(s["rt"], 5)
            v.reciprocal(su[:], su[:]).then_inc(s["rt"], 1)
            v.wait_ge(s["rt"], 6)
            tt(ex[:], ex[:], su[:].to_broadcast([TL, 2, EXPERTS]), ALU.mult).then_inc(s["rt"], 1)
            v.wait_ge(s["pe1"], 2)
            v.tensor_copy(wT[:], bank[6][0:EXPERTS, 0:TK]).then_inc(s["rt"], 1)
            v.wait_ge(s["pe1"], 4)
            for j in range(EJ):
                ins = v.tensor_copy(wb[:, j, :], bank[j][:, 0:TK])
            ins.then_inc(s["rt"], 1)
            v.tensor_copy(bw[:], bank[5][:, 0:TK]).then_inc(s["rt"], 1)
            v.wait_ge(s["rt"], 10)
            with v.Fori(0, STEPS) as i:
                for w in range(U):
                    h2 = H2[:, w % 4, :].rearrange("p (a t) -> p a t", t=TK)
                    v.wait_ge(s["act_2"], i * U + w + 1)
                    tt(h2, h2, wb[:, w // 2, :].unsqueeze(1).to_broadcast([P, GP, TK]), ALU.mult)\
                        .then_inc(s["wgt"], 1)
                v.wait_ge(s["mm3"], i * U + U)
                v.wait_ge(s["store"], i * 16 * GP + 16)
                tt(fo[:, 0, :], hflat[:, bass.ds(i * NCOL, NCOL)], bank[6][:, 0:NCOL], ALU.add).then_inc(s["res"], 1)
                v.wait_ge(s["res"], 2 * i + 2)
                f3 = fo[:, 0, :].rearrange("p (a t) -> p a t", t=TK)
                tt(f3, f3, bw[:].unsqueeze(1).to_broadcast([P, GP, TK]), ALU.add).then_inc(s["res"], 1)


def build(nc, d, hid, out):
    with ExitStack() as ctx:
        ssm_phase(nc, ctx, d["xT"], d["alog"], d["Dp"], d["Wb"], d["Wc"], d["Wr"], d["Wdt"], d["bdt"],
                  d["sel"], d["zsel"], hid)
    with ExitStack() as outer:
        hall = outer.enter_context(nc.sbuf_tensor("hall", [P, PAIRS, TK], F32))
        x2all = outer.enter_context(nc.sbuf_tensor("x2all", [P, PAIRS, TK], F32))
        with ExitStack() as ctx:
            mixer_phase(nc, ctx, d, hid, hall, x2all)
        with ExitStack() as ctx:
            expert_phase(nc, ctx, d, hall, x2all, out)


def layout(I):
    import numpy as np
    f = np.float32
    out = {}
    out["xT"] = np.ascontiguousarray(I["x"].reshape(32, 2, 750, 64).transpose(0, 1, 3, 2).reshape(32, 128, 750))

    def two(m):
        z = np.zeros((128, 128), f)
        z[0:64, 0:64] = m
        z[64:128, 64:128] = m
        return z

    W = I["L0_tok_W_dbc"]
    out["Wr"] = np.stack([two(np.repeat(W[l, 0:1, :].T, 64, 1)) for l in range(3)], 1)
    out["Wb"] = np.stack([two(W[l, 1:65, :].T) for l in range(3)], 1)
    out["Wc"] = np.stack([two(W[l, 65:129, :].T) for l in range(3)], 1)
    al = I["L0_tok_A_log"].transpose(2, 0, 1)
    out["alog"] = np.concatenate([al, al], 0)
    for k, s in (("Dp", "L0_tok_D"), ("bdt", "L0_tok_b_dt")):
        out[k] = np.concatenate([I[s].T, I[s].T], 0)
    w = I["L0_tok_W_dt"][:, :, 0].T
    out["Wdt"] = np.concatenate([w, w], 0)
    sel = np.zeros((3, 2, 16, 16, 2, 64), f)
    for b in range(2):
        for e in range(16):
            sel[:, b, e, e, b, :] = 1
    out["sel"] = sel.reshape(96, 16, 128)
    z = np.zeros((16, 8, 8, 112), f)
    for e in range(16):
        for q in range(8):
            z[e, q, q, 48 + e] = 0.5
    out["zsel"] = z.reshape(128, 8, 112)
    one = np.zeros((128, 128), f)
    one[0:64, 0:64] = one[64:, 64:] = 1
    out["ones"] = one
    out["ones64"] = one / np.float32(64)
    out["ident"] = np.eye(128, dtype=f)
    for k, n in (("wk", "W_k"), ("ww", "A_w"), ("wa", "A_a"), ("wr_", "W_r"), ("wv", "W_v"), ("wbw", "B_w"),
                 ("wba", "B_a"), ("wo", "W_o")):
        out[k] = two(I["L0_attn_" + n])
    out["wg"] = np.concatenate([I["L0_attn_A_g"]] * 2, 0)
    out["wbg"] = I["L0_attn_B_g"]
    vecs = list(I["L0_attn_x_mix"]) + [I["L0_attn_" + n] for n in ("b_w", "b_a", "k_k", "k_a", "r_k", "gn_w", "gn_b")]
    out["vec"] = np.concatenate([np.stack(vecs, 1)] * 2, 0)
    t = np.arange(96)
    same = (t[:, None] // 16 == t[None, :] // 16)
    before = same & (t[:, None] < t[None, :])
    upto = same & (t[:, None] <= t[None, :])
    out["m_lt"], out["m_l"] = -before.astype(f), -before.T.astype(f)
    out["m_ka"], out["m_kr"], out["m_br"] = before.astype(f), upto.astype(f), -upto.astype(f)
    out["cm"] = (t[:, None] // 16 == np.arange(6)[None, :]).astype(f)
    out["cmn"] = -out["cm"]
    e64 = np.eye(64, dtype=f)
    out["eye6"] = np.tile(e64, (2, 6))
    out["smask"] = np.tile((np.arange(384) % 16 != 0).astype(f), (128, 1))

    def ffn(n):
        return I["L0_ffn_" + n]

    w1 = np.zeros((128, 2, 4, 128), f)
    w2 = np.zeros((128, 4, 128), f)
    for j in range(4):
        for h in range(2):
            for b in range(2):
                w1[64 * b:64 * b + 64, b, j, 64 * h:64 * h + 64] = ffn("W1")[2 * j + h]
            w2[64 * h:64 * h + 64, j, 64 * h:64 * h + 64] = ffn("W2")[2 * j + h]
    out["fw1"], out["fw2"] = w1, w2
    out["fwo"] = ffn("Wo").reshape(4, 128, 64).transpose(1, 0, 2)
    out["fwr"] = np.concatenate([ffn("Wr")] * 2, 0)
    out["fbr"] = np.broadcast_to(ffn("br"), (96, 2, 8))
    out["fbo"] = np.concatenate([ffn("bo")] * 2, 1)
    fsel = np.zeros((8, 4, 2, 64), f)
    for j in range(4):
        for h in range(2):
            fsel[2 * j + h, j, h] = 1
    out["fsel"] = fsel.reshape(8, 4, 128)
    out["fbn"] = np.stack([np.stack([ffn(n + l).reshape(4, 128).T for n in ("b", "g", "be", "m", "v")], 1)
                           for l in "12"], 1)
    return {k: np.ascontiguousarray(v) for k, v in out.items()}


def kernel(**inputs):
    import numpy as np
    import concourse.bacc as bacc
    from concourse.bass_utils import run_bass_kernel_spmd as run
    nc = bacc.Bacc("TRN2", target_bir_lowering=False, num_devices=1)
    arrays = layout({k: np.asarray(v) for k, v in inputs.items()})
    d = {k: nc.dram_tensor("in_" + k, a.shape, mybir.dt.from_np(a.dtype), kind="ExternalInput").ap()
         for k, a in arrays.items()}
    hid = nc.dram_tensor("hidden", (32, 128, 187), F32, kind="Internal").ap()
    o = nc.dram_tensor("out_0", (32, 128, 187), F32, kind="ExternalOutput").ap()
    build(nc, d, hid, o)
    r = run(nc, [{"in_" + k: a for k, a in arrays.items()}], core_ids=[0])
    y = r.results[0]["out_0"]
    return np.ascontiguousarray(y.reshape(32, 2, 64, 187).transpose(0, 1, 3, 2).reshape(64, 187, 64))
```

```python
from contextlib import ExitStack

import concourse.bass as bass
from concourse import mybir

ALU = mybir.AluOpType
ACT = mybir.ActivationFunctionType
F32 = mybir.dt.float32
BF16 = mybir.dt.bfloat16
AX_X = mybir.AxisListType.X

P = 128
D = 64
T = [750, 375, 187]
Q = 8
TQ = [-(-t // Q) for t in T]
EG = 16
NG = D // EG
PAIRS = 32
HALF = PAIRS // 2
ITEMS = [(a, l) for l in range(3) for a in range(2)]
NI = len(ITEMS)
W = [1, 2, 4]
UPI = [D // w for w in W]
UNITS = sum(UPI[l] for _, l in ITEMS)
PREP = [[28, 30, 32, 34, 36, 38], [12, 14, 16, 18, 20, 22], [5, 6, 7, 9, 10, 12]]
WIDE = 375
STREAM = 96
NSPLIT = 3


def halves(l):
    return [(c, min(c + WIDE, T[l])) for c in range(0, T[l], WIDE)]


def pieces(l):
    n = TQ[l]
    parts = -(-n // 32)
    step = -(-n // parts)
    return [(k, min(k + step, n)) for k in range(0, n, step)]


def ubase(s):
    return sum(UPI[l] for _, l in ITEMS[:s])


ORDER = [(s, u) for s, (_, l) in enumerate(ITEMS) for u in range(UPI[l])]


def prep_tick(l, u):
    return PREP[l].index(u) if u in PREP[l] else None


def k_slots(l, last):
    parts = pieces(l)
    if last:
        cuts = {1: (0, 10), 2: (0, 4, 8), 3: (0, 4, 8, 10)}[len(parts)]
    else:
        cuts = {1: (0, 12), 2: (0, 6, 12), 3: (0, 5, 10, 15)}[len(parts)]
    out = [[] for _ in range(EG)]
    for j, (a, b) in enumerate(parts):
        per = -(-(b - a) // (cuts[j + 1] - cuts[j]))
        for slot, k in enumerate(range(a, b, per)):
            out[cuts[j] + slot].append((j, k, min(k + per, b)))
    return out


def evac_slots(l, last):
    end = {}
    for e, todo in enumerate(k_slots(l, last)):
        for j, _, _ in todo:
            end[j] = e
    return end


def ybank_schedule():
    order = []
    for s, (a, l) in enumerate(ITEMS):
        for h in range(len(halves(l))):
            order.append(("c", s, h))
        for h in range(2):
            order.append(("fin", (s - 1) % NI, h))
        n = (s + 1) % NI
        for w in ("z", "b"):
            for h in range(len(halves(ITEMS[n][1]))):
                order.append((w, n, h))
    return {u: i for i, u in enumerate(order)}


def bank_cuts(l):
    return [(0, 512), (512, T[l])] if T[l] > 512 else [(0, T[l])]


def ssm_phase(nc, ctx, xT, A_log, Dp, Wb, Wc, Wr, Wdt, bdt, sel_d, z_d, hid):
    sb = lambda n, s, d=F32: ctx.enter_context(nc.sbuf_tensor(n, s, d))
    ps = lambda n, s, d=F32: ctx.enter_context(nc.psum_tensor(n, s, d))
    sem = lambda n: ctx.enter_context(nc.semaphore(n))

    hst = sb("hst", [P, 2, EG * Q * TQ[0]])
    osb = sb("osb", [P, NG, TQ[0] * 2 * Q])
    RD = sb("RD", [96, 2, NG, T[0]], BF16)
    RU = sb("RU", [96, 2, NG, T[0]], BF16)
    xs = [sb(f"x{l}", [P, 2, T[l]]) for l in range(3)]
    Bs = sb("Bs", [P, 2, T[0]])
    Cb = sb("Cb", [P, TQ[0] * 2 * Q + STREAM])
    ub = sb("ub", [P, 2, T[0]])
    db = sb("db", [P, 2, T[0]])
    zz = sb("zz", [P, T[0]])
    ss = sb("ss", [P, T[0]])
    dp = sb("dp", [P, 3, T[0]], BF16)
    up = sb("up", [P, 3, T[0]], BF16)
    xf = sb("xf", [P, Q * TQ[0]])
    sel = sb("sel", [96, EG, P], BF16)
    zsel = sb("zsel", [P, Q, D + NG - 1])
    wb = sb("wb", [P, 3, P])
    wc = sb("wc", [P, 3, P])
    wr = sb("wr", [P, 3, P])
    A = sb("A", [P, 3, D])
    hd = sb("hd", [P, 3])
    wdt = sb("wdt", [P, 3])
    bd = sb("bd", [P, 3])

    pD = ps("pD", [P, 2, 1024])
    pU = ps("pU", [P, 1024])
    pO = ps("pO", [P, 512])
    pY = ps("pY", [P, 512])

    names = ("const", "aexp", "xload", "bcd", "bcu", "ucopy", "decay", "dbx", "scan", "ymm", "oev",
             "yfull", "cev", "bev", "zev", "zneg", "sp1", "sp", "dlt", "cast1", "res1", "cast2",
             "part", "rdl", "rul", "fin1", "fin", "hout", "mset", "selc")
    S = {n: sem("s_" + n) for n in names}
    yb = ybank_schedule()
    YN = len(yb)
    ZN = sum(len(halves(l)) for _, l in ITEMS)
    ON = sum(len(pieces(l)) for _, l in ITEMS) * NG

    def zcount(s):
        return sum(len(halves(l)) for _, l in ITEMS[:s])

    def ocount(s, g):
        return sum(len(pieces(l)) for _, l in ITEMS[:s]) * NG + g * len(pieces(ITEMS[s][1]))

    def zdone(n, h):
        return (zcount(n) if n else ZN) + h + 1

    ZPRE = len(halves(0))

    CONSTS = [(sel, sel_d), (zsel, z_d), (wb, Wb), (wc, Wc), (wr, Wr), (A, A_log), (hd, Dp), (wdt, Wdt), (bd, bdt)]

    def prev_group(s, g):
        return (s, g - 1) if g > 0 else ((s - 1) % NI, NG - 1)

    def turn(s):
        return (s + 1) % NI

    def products(s, g):
        return 0 if (s, g) == (NI - 1, NG - 1) else len(pieces(ITEMS[-1][1])) + ocount(s, g)

    def fin_bank(i, s, h, end):
        return i * YN + 2 * ZPRE + 1 + (h if end else yb[("fin", s, h)])

    with nc.Block() as block:
        @block.sync
        def _(sp):
            for dst, src in CONSTS[1:]:
                sp.dma_start(dst[:], src).then_inc(S["const"], 16)
            sp.dma_start(hst[0:96, 0, 0:EG * P], sel_d.rearrange("k e m -> k (e m)")).then_inc(S["hout"], 16)
            sp.dma_start(xs[0][:, 0, :], xT[0, :, :]).then_inc(S["xload"], 16)

            def waits(*pairs):
                for name, value in pairs:
                    sp.wait_ge(S[name], value)
                    sp.wait_ge(S["const"], 16 * (len(CONSTS) - 1))

            def restack(i, s, l, par):
                for src, dst, done in ((dp, RD, "rdl"), (up, RU, "rul")):
                    for r in range(3):
                        sp.dma_start(dst[32 * r:32 * r + 32, par, :, 0:T[l]], src[:, r, 0:T[l]])\
                            .then_inc(S[done], 16)

            sp.wait_ge(S["part"], 2)
            restack(0, 0, 0, 0)
            with sp.Fori(0, HALF) as i:
                i_b, i_a, i_h = sp.snap(i + HALF), sp.snap(i + 1), sp.snap(i + (HALF - 1))
                waits(("fin", i * NI + 1))
                sp.dma_start(xs[0][:, 1, :], xT[bass.ds(i_b, 1), :, :].rearrange("o p t -> p (o t)"))\
                    .then_inc(S["xload"], 16)
                for s in range(NI):
                    n = (s + 1) % NI
                    nl = ITEMS[n][1]
                    if s == 2:
                        waits(("fin", i * NI + 3))
                        sp.dma_start(xs[0][:, 0, :], xT[bass.ds(i_a, 1), :, :].rearrange("o p t -> p (o t)"))\
                            .then_inc(S["xload"], 16)
                    sp.wait_ge(S["part"], i * 2 * NI + 2 * (s + 2))
                    restack(i, n, nl, n % 2)
                    if s == 0:
                        waits(("fin", i * NI + 2))
                        sp.dma_start(hid[bass.ds(i_h, 1), :, :].rearrange("o p t -> p (o t)"), xs[2][:, 1, :])\
                            .then_inc(S["hout"], 16)
                    if s == 5:
                        waits(("fin", i * NI + 7))
                        sp.dma_start(hid[bass.ds(i, 1), :, :].rearrange("o p t -> p (o t)"), xs[2][:, 0, :])\
                            .then_inc(S["hout"], 16)
            waits(("fin", HALF * NI + 2))
            sp.dma_start(hid[PAIRS - 1, :, :], xs[2][:, 1, :]).then_inc(S["hout"], 16)
            sp.wait_ge(S["hout"], 16 * (2 * HALF + 2))

        @block.tensor
        def _(pe):
            def bank_free(i, use, end=False):
                k = yb[use]
                if k == 0 or end:
                    pe.wait_ge(S["bev"], i * ZN + ZPRE)
                    return
                kind, s, h = [u for u, n in yb.items() if n == k - 1][0]
                if kind == "c":
                    pe.wait_ge(S["cev"], i * ZN + zcount(s) + h + 1)
                elif kind == "fin":
                    pe.wait_ge(S["fin1"], i * 2 * NI + 2 * turn(s) + h + 2)
                else:
                    pe.wait_ge(S["zev" if kind == "z" else "bev"], i * ZN + zdone(s, h))

            def project(w, l, a, c0, c1):
                pe.matmul(pY[:, 0:c1 - c0], w[:, l, :], xs[l][:, a, c0:c1], start=True, stop=True)\
                    .then_inc(S["yfull"], 1)

            def y_step(i, s, g, l, todo):
                for j, k0, k1 in todo:
                    n = products(s, g) + j
                    if k0 == pieces(l)[0][0] and j == 0:
                        done = (ubase(s) + EG // W[l] * (g + 1)) % UNITS
                        pe.wait_ge(S["scan"], i * UNITS + done + 2)
                        if g == 0:
                            pe.wait_ge(S["cev"], i * ZN + zcount(s + 1))
                    if k0 == pieces(l)[j][0]:
                        pe.wait_ge(S["oev"], i * ON + n + 1)
                    par = g % 2
                    hv = hst[:, par, 0:EG * Q * TQ[l]]
                    for k in range(k0, k1):
                        c = 2 * Q * (k - pieces(l)[j][0])
                        n = min(STREAM, 512 - c)
                        last = pe.matmul(pO[:, c:c + n], hv[:, k:k + (P - 1) * TQ[l] + 1:TQ[l]],
                                         Cb[:, 2 * Q * k:2 * Q * k + n], start=True, stop=True)
                    if k1 == pieces(l)[j][1]:
                        last.then_inc(S["ymm"], 1)

            def fin_step(i, s, h, q, end=False):
                l = ITEMS[s][1]
                if q == 0:
                    if h == 1:
                        pe.wait_ge(S["fin1"], i * 2 * NI + 2 * turn(s) + 2)
                    else:
                        bank_free(i, ("fin", s, h), end)
                        pe.wait_ge(S["oev"], i * ON + products(s, NG - 1) + len(pieces(l)) + 1)
                ov = osb[:, :, 0:2 * Q * TQ[l]].rearrange("p g (k c) -> p g k c", c=2 * Q)
                for g in range(NG):
                    for b in range(2):
                        last = pe.matmul(pY[64 * b:64 * b + 64, q * TQ[l]:(q + 1) * TQ[l]],
                                         zsel[:, 4 * h + q, NG - 1 - g:NG - 1 - g + D], ov[:, g, :, 2 * (4 * h + q) + b],
                                         start=(g == 0), stop=(g == NG - 1))
                if q == 3:
                    last.then_inc(S["yfull"], 1)

            pe.wait_ge(S["const"], 16 * (len(CONSTS) - 1))
            pe.wait_ge(S["selc"], 1)
            pe.wait_ge(S["xload"], 16)
            for u, (c0, c1) in enumerate(halves(0)):
                if u:
                    pe.wait_ge(S["zev"], u)
                project(wr, 0, 0, c0, c1)
            for u, (c0, c1) in enumerate(halves(0)):
                pe.wait_ge(S["bev" if u else "zev"], u or ZPRE)
                project(wb, 0, 0, c0, c1)

            pe.wait_ge(S["mset"], 3)
            with pe.Fori(0, HALF) as i:
                def channels(s, u):
                    l = ITEMS[s][1]
                    w, step = W[l], 1024 // W[l]
                    g, e0 = w * u // EG, w * u % EG
                    K = ubase(s) + u
                    if u == 0:
                        pe.wait_ge(S["rdl"], (i * NI + s + 1) * 16 * NSPLIT)
                        pe.wait_ge(S["rul"], (i * NI + s + 1) * 16 * NSPLIT)
                    pe.wait_ge(S["ucopy"], i * UNITS + K + 1)
                    for j in range(w):
                        for c0, c1 in bank_cuts(l):
                            last = pe.matmul(pU[:, step * j + c0:step * j + c1], sel[:, e0 + j, :],
                                             RU[:, s % 2, g, c0:c1], start=True, stop=True)
                    last.then_inc(S["bcu"], 1)
                    pe.wait_ge(S["scan"], i * UNITS + K + 1)
                    for j in range(w):
                        for c0, c1 in bank_cuts(l):
                            last = pe.matmul(pD[:, u % 2, step * j + c0:step * j + c1], sel[:, e0 + j, :],
                                             RD[:, s % 2, g, c0:c1], start=True, stop=True)
                    last.then_inc(S["bcd"], 1)

                def beside(s, u):
                    a, l = ITEMS[s]
                    n = (s + 1) % NI
                    na, nl = ITEMS[n]
                    hn = halves(nl)
                    w, step = W[l], 1024 // W[l]
                    g, e0 = w * u // EG, w * u % EG
                    for e in range(e0, e0 + w):
                        ys, yg = prev_group(s, g)
                        y_step(i, ys, yg, ITEMS[ys][1], k_slots(ITEMS[ys][1], yg == NG - 1)[e])
                        if g == 0 and e in (10, 12) and (e - 10) // 2 < len(halves(l)):
                            bank_free(i, ("c", s, (e - 10) // 2))
                            project(wc, l, a, *halves(l)[(e - 10) // 2])
                        if g == 0 and e >= 14:
                            for q in range(2):
                                fin_step(i, (s - 1) % NI, 0, 2 * (e - 14) + q)
                        if g == 1 and e in (2, 3):
                            for q in range(2):
                                fin_step(i, (s - 1) % NI, 1, 2 * (e - 2) + q)
                    k = prep_tick(l, u)
                    if k in (0, 1) and k < len(hn):
                        if k == 0:
                            if nl == 0:
                                pe.wait_ge(S["xload"], 16 * (2 * i + (2 if n == 1 else 3)))
                            else:
                                pe.wait_ge(S["fin"], i * NI + n + 1)
                        bank_free(i, ("z", n, k))
                        project(wr, nl, na, *hn[k])
                    if k in (3, 4) and k - 3 < len(hn):
                        bank_free(i, ("b", n, k - 3))
                        project(wb, nl, na, *hn[k - 3])

                for k, unit in enumerate(ORDER):
                    channels(*unit)
                    if k > 0:
                        beside(*ORDER[k - 1])
                beside(*ORDER[-1])
            s = NI - 1
            for todo in k_slots(ITEMS[s][1], True):
                y_step(HALF, s, NG - 1, ITEMS[s][1], todo)
            for h in range(2):
                for q in range(4):
                    fin_step(HALF, s, h, q, end=True)

        @block.scalar
        def _(act):
            def softplus(l, prep):
                act.wait_ge(S["zneg"], prep)
                act.activation(ss[:, 0:T[l]], ss[:, 0:T[l]], ACT.Exp).then_inc(S["sp1"], 1)
                act.wait_ge(S["sp1"], prep)
                act.activation(ss[:, 0:T[l]], ss[:, 0:T[l]], ACT.Ln, bias=1.0).then_inc(S["sp"], 1)

            def cast(l, part, src_done, counter, prep, again=True):
                for k, (dst, src) in enumerate(((dp, ss), (up, zz))):
                    act.wait_ge(S[src_done], 2 * prep - 1 + k)
                    if part == 0 and again:
                        act.wait_ge(S["rdl" if k == 0 else "rul"], (prep - 1) * 16 * NSPLIT)
                    act.activation(dst[:, part, 0:T[l]], src[:, 0:T[l]], ACT.Copy).then_inc(S[counter], 1)

            def b_half(par, c0, c1, full_count):
                act.wait_ge(S["yfull"], full_count)
                act.activation(Bs[:, par, c0:c1], pY[:, 0:c1 - c0], ACT.Copy).then_inc(S["bev"], 1)

            def o_evac(i, s, g, j):
                l = ITEMS[s][1]
                k0, k1 = pieces(l)[j]
                act.wait_ge(S["ymm"], i * ON + products(s, g) + j + 1)
                if g == 0 and j == 0:
                    act.wait_ge(S["yfull"], fin_bank(i, (s - 1) % NI, 1, False))
                act.activation(osb[:, g, 2 * Q * k0:2 * Q * k1], pO[:, 0:2 * Q * (k1 - k0)], ACT.Copy)\
                    .then_inc(S["oev"], 1)

            def c_half(i, s, h, c0, c1):
                l = ITEMS[s][1]
                act.wait_ge(S["yfull"], i * YN + yb[("c", s, h)] + 2 * ZPRE + 1)
                cv = Cb[:, 0:2 * Q * TQ[l]].rearrange("p (k q b) -> p b q k", q=Q, b=2)
                tq = TQ[l]
                last = None
                runs = []
                q0, q1 = -(-c0 // tq), c1 // tq
                if c0 < q0 * tq:
                    runs.append((c0, q0 * tq))
                if q1 > q0:
                    runs.append((q0 * tq, q1 * tq))
                if q1 * tq < c1:
                    runs.append((q1 * tq, c1))
                for b in range(2):
                    for r0, r1 in runs:
                        pp = slice(64 * b, 64 * b + 64)
                        if (r1 - r0) > tq or (r1 - r0 == tq and r0 % tq == 0):
                            dst = cv[pp, b, r0 // tq:r1 // tq, :]
                            src = pY[pp, r0 - c0:r1 - c0].rearrange("p (q k) -> p q k", k=tq)
                        else:
                            q = r0 // tq
                            dst = cv[pp, b, q, r0 - q * tq:r1 - q * tq]
                            src = pY[pp, r0 - c0:r1 - c0]
                        last = act.activation(dst, src, ACT.Copy)
                last.then_inc(S["cev"], 1)

            act.wait_ge(S["hout"], 16)
            act.activation(sel[:].rearrange("k e m -> k (e m)"), hst[0:96, 0, 0:EG * P], ACT.Copy).then_inc(S["selc"], 1)
            act.preload_act_table_set("natural_log_exp_and_others")
            act.wait_ge(S["const"], 16 * (len(CONSTS) - 1))
            act.wait_ge(S["mset"], 3)
            act.activation(A[:], A[:], ACT.Exp).then_inc(S["aexp"], 1)
            act.wait_ge(S["aexp"], 1)
            act.activation(A[:], A[:], ACT.Copy, scale=-1.0).then_inc(S["aexp"], 1)
            act.wait_ge(S["aexp"], 2)
            act.activation(hd[:], hd[:], ACT.Copy, scale=0.5).then_inc(S["aexp"], 1)
            act.activation(ub[0:1, 0, 0:1], bd[0:1, 0:1], ACT.Copy).then_inc(S["ucopy"], 1)
            act.wait_ge(S["ucopy"], 1)
            act.activation(osb[0:1, 0, 0:1], bd[0:1, 0:1], ACT.Copy).then_inc(S["oev"], 1)
            act.wait_ge(S["oev"], 1)
            act.wait_ge(S["aexp"], 3)

            def evac_z(l, c0, c1, full_count, prep):
                if prep is not None:
                    act.wait_ge(S["part"], 2 * (prep - 1))
                act.wait_ge(S["yfull"], full_count)
                act.activation(zz[:, c0:c1], pY[:, 0:c1 - c0], ACT.Identity, scale=wdt[:, l:l + 1],
                               bias=bd[:, l:l + 1]).then_inc(S["zev"], 1)

            for u, (c0, c1) in enumerate(halves(0)):
                evac_z(0, c0, c1, u + 1, None)
            softplus(0, 1)
            cast(0, 0, "dlt", "cast1", 1, again=False)
            cast(0, 1, "res1", "cast2", 1, again=False)
            for u, (c0, c1) in enumerate(halves(0)):
                b_half(0, c0, c1, ZPRE + u + 1)

            with act.Fori(0, HALF) as i:
                def channels(s, u):
                    l = ITEMS[s][1]
                    w, step = W[l], 1024 // W[l]
                    g, e0 = w * u // EG, w * u % EG
                    K = ubase(s) + u
                    act.wait_ge(S["bcu"], i * UNITS + K + 1)
                    act.wait_ge(S["dbx"], i * UNITS + K + 1)
                    act.activation(ub[:, u % 2, 0:w * T[l]].rearrange("p (w t) -> p w t", w=w),
                                   pU[:].rearrange("p (w t) -> p w t", w=w)[:, :, 0:T[l]], ACT.Copy)\
                        .then_inc(S["ucopy"], 1)
                    act.wait_ge(S["bcd"], i * UNITS + K + 1)
                    for j in range(w):
                        pd = pD[:, u % 2, step * j:step * j + T[l]]
                        c = NG * (e0 + j) + g
                        last = act.activation(pd, pd, ACT.Exp, scale=A[:, l, c:c + 1])
                    last.then_inc(S["decay"], 1)

                def beside(s, u):
                    l = ITEMS[s][1]
                    n = (s + 1) % NI
                    nl = ITEMS[n][1]
                    hn = halves(nl)
                    w = W[l]
                    g, e0 = w * u // EG, w * u % EG
                    for e in range(e0, e0 + w):
                        ys, yg = prev_group(s, g)
                        for j, at in evac_slots(ITEMS[ys][1], yg == NG - 1).items():
                            if at == e:
                                o_evac(i, ys, yg, j)
                        if g == 0 and e in (10, 12) and (e - 10) // 2 < len(halves(l)):
                            c_half(i, s, (e - 10) // 2, *halves(l)[(e - 10) // 2])
                    prep = i * NI + s + 2
                    k = prep_tick(l, u)
                    if k in (1, 2) and k - 1 < len(hn):
                        evac_z(nl, *hn[k - 1], i * YN + yb[("z", n, k - 1)] + 2 * ZPRE + 1, prep)
                    if k == 3:
                        softplus(nl, prep)
                    if k == 4:
                        cast(nl, 0, "dlt", "cast1", prep)
                    if k == 5:
                        cast(nl, 1, "res1", "cast2", prep)
                    if k in (4, 5) and k - 4 < len(hn):
                        b_half(n % 2, *hn[k - 4], i * YN + yb[("b", n, k - 4)] + 2 * ZPRE + 1)

                for k, unit in enumerate(ORDER):
                    channels(*unit)
                    if k > 0:
                        beside(*ORDER[k - 1])
                beside(*ORDER[-1])
            for j in range(len(pieces(ITEMS[-1][1]))):
                o_evac(HALF, NI - 1, NG - 1, j)

        @block.gpsimd
        def _(pool):
            def residual(l, prep):
                pool.wait_ge(S["dlt"], 2 * prep)
                for k, (src, p) in enumerate(((ss, dp), (zz, up))):
                    pool.wait_ge(S["cast1"], 2 * prep - 1 + k)
                    pool.tensor_tensor(src[:, 0:T[l]], src[:, 0:T[l]], p[:, 0, 0:T[l]], ALU.subtract)\
                        .then_inc(S["res1"], 1)

            def third(l, prep):
                for k, (src, p) in enumerate(((ss, dp), (zz, up))):
                    pool.wait_ge(S["cast2"], 2 * prep - 1 + k)
                    pool.wait_ge(S["res1"], 2 * prep - 1 + k)
                    pool.tensor_tensor(p[:, 2, 0:T[l]], src[:, 0:T[l]], p[:, 1, 0:T[l]], ALU.subtract)\
                        .then_inc(S["part"], 1)

            pool.memset(db[:, 0, :], 0.0).then_inc(S["dbx"], 1)
            pool.memset(db[:, 1, :], 0.0).then_inc(S["dbx"], 1)
            pool.wait_ge(S["dbx"], 2)
            pool.memset(osb[:], 0.0).then_inc(S["mset"], 1)
            pool.memset(xs[2][:], 0.0).then_inc(S["mset"], 1)
            residual(0, 1)
            third(0, 1)
            with pool.Fori(0, HALF) as i:
                def channels(s, u):
                    l = ITEMS[s][1]
                    w = W[l]
                    K = ubase(s) + u
                    if u == 0:
                        pool.wait_ge(S["bev"], i * ZN + zcount(s + 1))
                    pool.wait_ge(S["ucopy"], i * UNITS + K + 2)
                    pool.wait_ge(S["scan"], i * UNITS + K + 1)
                    view = lambda b: b[:, u % 2, 0:w * T[l]].rearrange("p (w t) -> p w t", w=w)
                    pool.tensor_tensor(view(db), view(ub),
                                       Bs[:, s % 2, 0:T[l]].unsqueeze(1).to_broadcast([P, w, T[l]]),
                                       ALU.mult).then_inc(S["dbx"], 1)

                def beside(s, u):
                    l = ITEMS[s][1]
                    n = (s + 1) % NI
                    nl = ITEMS[n][1]
                    k = prep_tick(l, u)
                    if k == 4:
                        residual(nl, i * NI + s + 2)
                    if k == 5:
                        third(nl, i * NI + s + 2)

                for k, unit in enumerate(ORDER):
                    channels(*unit)
                    if k > 0:
                        beside(*ORDER[k - 1])
                beside(*ORDER[-1])

        @block.vector
        def _(v):
            def negabs(l, halves_done):
                v.wait_ge(S["zev"], halves_done)
                v.scalar_tensor_tensor(ss[:, 0:T[l]], zz[:, 0:T[l]], -1.0, zz[:, 0:T[l]], ALU.mult, ALU.min)\
                    .then_inc(S["zneg"], 1)

            def delta_u(l, a, prep):
                v.wait_ge(S["sp"], prep)
                v.scalar_tensor_tensor(ss[:, 0:T[l]], zz[:, 0:T[l]], 0.0, ss[:, 0:T[l]], ALU.max, ALU.add)\
                    .then_inc(S["dlt"], 1)
                v.wait_ge(S["dlt"], 2 * prep - 1)
                v.tensor_tensor(zz[:, 0:T[l]], ss[:, 0:T[l]], xs[l][:, a, :], ALU.mult).then_inc(S["dlt"], 1)

            def fin(i, s, h, end=False):
                a, l = ITEMS[s]
                c0, c1 = 4 * h * TQ[l], min(4 * (h + 1) * TQ[l], T[l])
                v.wait_ge(S["yfull"], fin_bank(i, s, h, end))
                v.scalar_tensor_tensor(xf[:, c0:c1], xs[l][:, a, c0:c1], hd[:, l:l + 1], pY[:, 0:c1 - c0],
                                       ALU.mult, ALU.add).then_inc(S["fin1"], 1)
                if h == 1:
                    v.wait_ge(S["fin1"], 2 * (i * NI + turn(s) + 1) + 1)
                    if l < 2:
                        m = T[l + 1]
                        xv = xf[:, 0:2 * m].rearrange("p (t two) -> p two t", two=2)
                        if l == 1:
                            v.wait_ge(S["hout"], 16 * (2 * i + 1 + a))
                        v.tensor_tensor(xs[l + 1][:, a, :], xv[:, 0, :], xv[:, 1, :], ALU.add).then_inc(S["fin"], 1)
                    else:
                        v.tensor_scalar(xs[2][:, a, :], xf[:, 0:T[2]], 2.0, None, ALU.mult).then_inc(S["fin"], 1)

            v.wait_ge(S["selc"], 1)
            v.memset(hst[:, 0, :], 0.0).then_inc(S["scan"], 1)
            v.memset(hst[:, 1, :], 0.0).then_inc(S["scan"], 1)
            v.memset(Cb[:], 0.0).then_inc(S["mset"], 1)
            v.memset(xf[:, 0:1], 0.0).then_inc(S["fin"], 1)
            v.memset(xf[:, 1:2], 0.0).then_inc(S["fin1"], 1)
            v.wait_ge(S["scan"], 2)
            v.wait_ge(S["mset"], 1)
            negabs(0, len(halves(0)))
            v.wait_ge(S["xload"], 16)
            delta_u(0, 0, 1)
            v.wait_ge(S["aexp"], 3)
            v.wait_ge(S["mset"], 3)
            with v.Fori(0, HALF) as i:
                def channels(s, u):
                    l = ITEMS[s][1]
                    TP = Q * TQ[l]
                    w, step = W[l], 1024 // W[l]
                    g, e0 = w * u // EG, w * u % EG
                    K = ubase(s) + u
                    if e0 == 0:
                        v.wait_ge(S["oev"], i * ON + products(*prev_group(s, g)) + 1)
                    v.wait_ge(S["decay"], i * UNITS + K + 1)
                    v.wait_ge(S["dbx"], i * UNITS + K + 3)
                    for j in range(w):
                        last = v.tensor_tensor_scan(
                            hst[:, g % 2, (e0 + j) * TP:(e0 + j) * TP + T[l]],
                            pD[:, u % 2, step * j:step * j + T[l]],
                            db[:, u % 2, j * T[l]:(j + 1) * T[l]], 0.0, ALU.mult, ALU.add)
                    last.then_inc(S["scan"], 1)

                def beside(s, u):
                    l = ITEMS[s][1]
                    n = (s + 1) % NI
                    na, nl = ITEMS[n]
                    w = W[l]
                    g, e0 = w * u // EG, w * u % EG
                    for e in range(e0, e0 + w):
                        if g == 0 and e == 15:
                            fin(i, (s - 1) % NI, 0)
                        if g == 1 and e == 3:
                            fin(i, (s - 1) % NI, 1)
                    k = prep_tick(l, u)
                    if k == 2:
                        negabs(nl, i * ZN + zdone(n, len(halves(nl)) - 1))
                    if k == 3:
                        delta_u(nl, na, i * NI + s + 2)

                for k, unit in enumerate(ORDER):
                    channels(*unit)
                    if k > 0:
                        beside(*ORDER[k - 1])
                beside(*ORDER[-1])
            for h in range(2):
                fin(HALF, NI - 1, h, end=True)



TK = 192
CH = 16
TL = 96
NC = TK // CH
CT = TL // CH
GP = 2
NCOL = GP * TK
NT_ = GP * TK // TL
NU = 2 * NT_
STEPS = PAIRS // GP
TR = T[2]
DECAY = -0.6065306597126334
MIX = ("r", "w", "k", "v", "a", "g")
EXPERTS = 8
EJ = EXPERTS // 2


class Steps:

    def __init__(self, sem, names):
        self.sem, self.names, self.at, self.n = sem, names, {n: k + 1 for k, n in enumerate(names)}, len(names)

    def value(self, i, name):
        return i * self.n + self.at[name]


def mixer_phase(nc, ctx, W, hid, hall, x2all):
    sb = lambda n, s, d=F32: ctx.enter_context(nc.sbuf_tensor(n, s, d))
    sem = lambda n: ctx.enter_context(nc.semaphore(n))
    bank = [ctx.enter_context(nc.psum_tensor(f"bank{k}", [P, 512], F32)) for k in range(8)]
    F = lambda n: sb(n, [P, NCOL])

    const = {k: sb("c_" + k, list(W[k].shape), F32) for k in
             ("ones", "ones64", "ident", "wk", "ww", "wa", "wr_", "wv", "wg", "wbw", "wba", "wbg", "wo",
              "vec", "m_lt", "m_l", "m_ka", "m_kr", "m_br", "cm", "cmn", "eye6", "smask")}
    c = const
    VEC = {n: k for k, n in enumerate(("mix_r", "mix_w", "mix_k", "mix_v", "mix_a", "mix_g", "b_w", "b_a", "k_k",
                                       "k_a", "r_k", "gn_w", "gn_b"))}
    vec = lambda n: c["vec"][:, VEC[n]:VEC[n] + 1]
    cst = sb("cst", [P, 4])
    xc, sq, rs, dx, t1, t2, ha, aa = (F(n) for n in ("xc", "sq", "rs", "dx", "t1", "t2", "ha", "aa"))
    xp = sb("xp", [P, GP, TK + 1])
    xm = {m: F("xm_" + m) for m in MIX}
    kk, kp, bb, ww, cs, al, be, ka, rho, rk, vF, bon, gF = (
        F(n) for n in ("kk", "kp", "bb", "ww", "cs", "al", "be", "ka", "rho", "rk", "vF", "bon", "gF"))
    Pi, Pn, Pe = xm["w"], xm["a"], xm["k"]
    oF, oc = xm["r"], xm["v"]
    gh = sb("gh", [P, 2, NCOL])
    VN, bN, kN = (sb(n, [TL, NT_, P]) for n in ("VN", "bN", "kN"))
    Y = sb("Y", [TL, NT_, 2, P])
    mats = {n: sb("g_" + n, [TL, NU, TL]) for n in ("NT", "N", "KA", "KR", "BR", "N2T", "N2", "N4T", "N4", "N8T")}
    bX, vX, uX = (sb(n, [TL, NT_, 2, CT, D]) for n in ("bX", "vX", "uX"))
    GT, HP = (sb(n, [P, NT_, CT * D]) for n in ("GT", "HP"))
    M = sb("M", [P, NC, GP, D])

    s_const, s_h, s_set = sem("m_const"), sem("m_h"), sem("m_set")
    PE = Steps(sem("m_pe"), ["mean", "var", "k", "hw", "ha", "r", "vF", "vN", "hg0", "hg1", "w", "a", "ss", "bsum",
                             "tA", "tB", "tK", "LT", "L", "KA", "KR", "BR", "LKV", "Y1a", "Y1b", "N2T", "N2", "Y2a",
                             "Y2b", "N4T", "N4", "Y3a", "Y3b", "N8T", "Y4a", "Y4b"]
               + ["GT%d" % k for k in range(NT_)] + ["HP%d" % k for k in range(NT_)] + ["RT"]
               + ["M%d" % k for k in range(2, NC)] + ["g", "O", "omean", "ovar", "out", "mean2", "var2"])
    AC = Steps(sem("m_act"), ["lnv", "rstd", "ew", "hac", "vFc", "VN", "eg0", "eg1", "ew2", "ea", "lnk", "rk",
                              "Pi", "Pn", "Pe", "aN", "bN", "kN", "LKV", "N2T", "N2", "N4T", "N4", "N8T",
                              "gF", "oF", "lno", "rstdo", "lnv2", "rstd2"])
    DV = Steps(sem("m_dve"), ["xc", "sq", "x", "dx"] + ["mix_" + m for m in ("k", "w", "a", "r", "v", "g")]
               + ["w1", "w2", "w3", "s1", "s2", "s3", "a1", "a2", "kk", "kk2", "ssm", "kkn", "ka1", "kp", "b",
                  "cs", "ce", "al", "be", "ka", "rho", "rk", "bon", "g", "NT", "g0", "N", "g1", "KA", "g2", "KR", "g3", "BR",
                  "g4", "Y1a", "Y1b", "g5", "Y2a", "Y2b", "g6", "Y3a", "Y3b", "g7", "Y4a", "Y4b", "uX"]
               + ["GT%d" % k for k in range(NT_)] + ["HP%d" % k for k in range(NT_)] + ["RT", "M1"]
               + ["M%d" % k for k in range(2, NC)]
               + ["oc", "osq", "on1", "on2", "on3", "on4", "hn", "xc2", "sq2", "x2"])
    PL = Steps(sem("m_pool"), ["bX", "vX"])

    class On:

        def __init__(self, eng, own, i):
            self.eng, self.own, self.i, self.k = eng, own, i, 0

        def need(self, steps, *names):
            last = max(names, key=lambda n: steps.at[n])
            self.eng.wait_ge(steps.sem, steps.value(self.i, last))

        def step(self, name, ins):
            assert self.own.names[self.k] == name, (self.own.names[self.k], name)
            self.k += 1
            ins.then_inc(self.own.sem, 1)

    def cols(i):
        return bass.ds(i * NCOL, NCOL)

    hflat = hall[:].rearrange("p a t -> p (a t)")
    xflat = x2all[:].rearrange("p a t -> p (a t)")
    pr = lambda t: t[:].rearrange("p (a t) -> p a t", t=TK)
    unit4 = lambda b: bank[b][0:TL, 0:4 * TL].rearrange("p (u t) -> p u t", t=TL)

    with nc.Block() as block:
        @block.sync
        def _(sp):
            for k in const:
                sp.dma_start(const[k][:], W[k]).then_inc(s_const, 16)
            sp.wait_ge(s_set, 4)
            for p in range(PAIRS):
                sp.dma_start(hall[:, p, 0:TR], hid[p, :, :]).then_inc(s_h, 16)

        @block.gpsimd
        def _(pool):
            pool.memset(hall[:], 0.0).then_inc(s_set, 1)
            pool.memset(cst[:, 0:1], 1e-5).then_inc(s_set, 1)
            pool.memset(cst[:, 1:2], D * 1e-5).then_inc(s_set, 1)
            pool.memset(cst[:, 2:3], 15 * 0.6931471805599453).then_inc(s_set, 1)
            pool.wait_ge(s_const, 16 * len(const))
            with pool.Fori(0, STEPS) as i:
                o = On(pool, PL, i)
                for name, src, dst in (("bX", bN, bX), ("vX", VN, vX)):
                    o.need(AC, "bN" if name == "bX" else "VN")
                    for k in range(NT_):
                        ins = pool.tensor_tensor(dst[:, k], src[:, k, :].rearrange("p (b f) -> p b f", b=2)
                                                 .unsqueeze(2).to_broadcast([TL, 2, CT, D]),
                                                 c["cm"][:].unsqueeze(1).unsqueeze(3).to_broadcast([TL, 2, CT, D]),
                                                 ALU.mult)
                    o.step(name, ins)

        @block.tensor
        def _(pe):
            pe.wait_ge(s_const, 16 * len(const))
            pe.wait_ge(s_h, 16 * PAIRS)
            with pe.Fori(0, STEPS) as i:
                o = On(pe, PE, i)
                mm = lambda out, l, r, a=True, z=True: pe.matmul(out, l, r, start=a, stop=z)
                full = lambda b: bank[b][:, 0:NCOL]
                pe.wait_ge(DV.sem, i * DV.n)
                o.step("mean", mm(full(0), c["ones64"][:], hflat[:, cols(i)]))
                o.need(DV, "sq")
                o.step("var", mm(full(1), c["ones64"][:], sq[:]))
                for name, b, w, m in (("k", 2, "wk", "k"), ("hw", 3, "ww", "w"), ("ha", 4, "wa", "a"),
                                      ("r", 5, "wr_", "r"), ("vF", 6, "wv", "v")):
                    o.need(DV, "mix_" + m)
                    o.step(name, mm(full(b), c[w][:], xm[m][:]))
                for k in range(NT_):
                    ins = mm(bank[7][0:TL, P * k:P * k + P], xm["v"][:, TL * k:TL * k + TL], c["wv"][:])
                o.step("vN", ins)
                o.need(DV, "mix_g")
                o.need(AC, "lnv")
                for b in range(2):
                    o.step("hg%d" % b, mm(full(b), c["wg"][64 * b:64 * b + 64, :], xm["g"][64 * b:64 * b + 64, :]))
                o.need(DV, "w3")
                o.step("w", mm(full(3), c["wbw"][:], t1[:]))
                o.need(AC, "hac")
                o.step("a", mm(full(4), c["wba"][:], ha[:]))
                o.need(DV, "kk2")
                o.step("ss", mm(full(1), c["ones"][:], sq[:]))
                o.need(DV, "rk")
                o.step("bsum", mm(full(5), c["ones"][:], rk[:]))
                for name, b, src, free in (("tA", 6, al, (AC, "vFc")), ("tB", 7, be, (AC, "VN")),
                                           ("tK", 2, ka, (DV, "kp"))):
                    o.need(*free)
                    for k in range(NT_):
                        ins = pe.transpose(bank[b][0:TL, P * k:P * k + P], src[:, TL * k:TL * k + TL], c["ident"][:])
                    o.step(name, ins)
                for name, (l, r), b0, free in (
                        ("LT", (be, al), 3, ((AC, "ew2"), (AC, "ea"))), ("L", (al, be), 0, ((AC, "eg1"), (DV, "ssm"))),
                        ("KA", (ka, al), 3, ((DV, "NT"),)), ("KR", (ka, rho), 0, ((DV, "N"),)),
                        ("BR", (be, rho), 3, ((DV, "KA"),))):
                    for f in free:
                        o.need(*f)
                    for u in range(NU):
                        b, k = divmod(u, NT_)
                        sl = slice(64 * b, 64 * b + 64)
                        ins = mm(unit4(b0 + b)[:, k, :], l[sl, TL * k:TL * k + TL],
                                 r[sl, TL * k:TL * k + TL])
                    o.step(name, ins)
                o.need(DV, "KA", "bon")
                o.need(AC, "VN")
                for u in range(NU):
                    k, b = divmod(u, 2)
                    ins = mm(bank[5][0:TL, D * u:D * u + D], mats["KA"][:, NT_ * b + k, :], VN[:, k, 64 * b:64 * b + 64])
                o.step("LKV", ins)

                def apply(mat, tag):
                    for h, x in enumerate("ab"):
                        for u in range(4 * h, 4 * h + 4):
                            k, b = divmod(u, 2)
                            ins = mm(bank[6 + h][0:TL, P * (u % 4):P * (u % 4) + P], mats[mat][:, NT_ * b + k, :], Y[:, k, b, :])
                        o.step(tag + x, ins)

                def square(name, l, r, b0):
                    for u in range(NU):
                        ins = mm(unit4(b0 + u // 4)[:, u % 4, :], mats[l][:, u, :], mats[r][:, u, :])
                    o.step(name, ins)

                o.need(AC, "LKV", "aN", "bN")
                apply("NT", "Y1")
                o.need(DV, "BR")
                square("N2T", "N", "NT", 3)
                square("N2", "NT", "N", 0)
                o.need(AC, "N2")
                o.need(DV, "Y1b")
                apply("N2T", "Y2")
                square("N4T", "N2", "N2T", 3)
                square("N4", "N2T", "N2", 0)
                o.need(AC, "N4")
                o.need(DV, "Y2b")
                apply("N4T", "Y3")
                square("N8T", "N4", "N4T", 3)
                o.need(AC, "N8T")
                o.need(DV, "Y3b")
                apply("N8T", "Y4")
                o.need(DV, "Y4b")
                o.need(PL, "bX")
                for k in range(NT_):
                    for b in range(2):
                        ins = mm(bank[k][64 * b:64 * b + 64, 0:CT * D], Y[:, k, b, 0:D],
                                 bX[:, k, b].rearrange("p c f -> p (c f)"))
                    o.step("GT%d" % k, ins)
                o.need(DV, "uX")
                o.need(PL, "vX")
                for k in range(NT_):
                    for b in range(2):
                        out = bank[4 + k][64 * b:64 * b + 64, 0:CT * D]
                        mm(out, kN[:, k, 64 * b:64 * b + 64], vX[:, k, b].rearrange("p c f -> p (c f)"), True, False)
                        ins = mm(out, bN[:, k, 64 * b:64 * b + 64], uX[:, k, b].rearrange("p c f -> p (c f)"),
                                 False, True)
                    o.step("HP%d" % k, ins)
                o.need(DV, "GT0")
                for u in range(NU):
                    k, b = divmod(u, 2)
                    ins = mm(bank[0][64 * b:64 * b + 64, TL * k:TL * k + TL], Y[:, k, b, 0:D], mats["BR"][:, NT_ * b + k, :])
                o.step("RT", ins)
                def add_tile(k):
                    for b in range(2):
                        out = bank[3 + k][64 * b:64 * b + 64, 0:TL]
                        mm(out, VN[:, k, 64 * b:64 * b + 64], mats["KR"][:, NT_ * b + k, :], True, False)
                        if (k, b) != (NT_ - 1, 1):
                            mm(out, Y[:, k, b, D:P], mats["BR"][:, NT_ * b + k, :], False, False)

                def read_state(ci):
                    half, cc = divmod(ci, CT)
                    for p in range(GP):
                        for b in range(2):
                            sl = slice(64 * b, 64 * b + 64)
                            k = 2 * p + half
                            ins = mm(bank[3 + k][sl, CH * cc:CH * cc + CH], M[sl, ci, p, :],
                                     al[sl, TL * k + CH * cc:TL * k + CH * cc + CH], False, cc == CT - 1)
                    return ins

                beside = {1: ((0,), ()), 2: ((2,), ()), 3: ((), (1, 2)), 4: ((), (3, 4)), 5: ((1,), (5,)), 6: ((3,), ()),
                          7: ((), (6, 7)), 8: ((), (8,)), 9: ((), (9,)), 10: ((), (10,))}
                o.need(DV, "HP3")
                for ci in range(1, NC - 1):
                    o.need(DV, "M%d" % ci)
                    half, cc = divmod(ci, CT)
                    mm(bank[1 + ci % 2][:, 0:GP * D], c["ident"][:],
                       HP[:].rearrange("p (a h) (c f) -> p a h c f", h=2, f=D)[:, :, half, cc, :], True, False)
                    for p in range(GP):
                        for b in range(2):
                            sl = slice(64 * b, 64 * b + 64)
                            ins = mm(bank[1 + ci % 2][sl, D * p:D * p + D], GT[sl, 2 * p + half, D * cc:D * cc + D],
                                     M[sl, ci, p, :], False, p == GP - 1)
                    o.step("M%d" % (ci + 1), ins)
                    for k in beside[ci][0]:
                        add_tile(k)
                    for state in beside[ci][1]:
                        read_state(state)
                for b in range(2):
                    ins = mm(bank[0][64 * b:64 * b + 64, 0:NCOL], c["wbg"][:], gh[:, b, :])
                o.step("g", ins)
                o.need(DV, "M%d" % (NC - 1))
                mm(bank[3 + NT_ - 1][64:P, 0:TL], Y[:, NT_ - 1, 1, D:P], mats["BR"][:, NU - 1, :], False, False)
                o.step("O", read_state(NC - 1))
                o.need(AC, "oF")
                o.step("omean", mm(full(4), c["ones64"][:], oF[:]))
                o.need(DV, "osq")
                o.step("ovar", mm(full(5), c["ones64"][:], sq[:]))
                o.need(DV, "on4")
                o.step("out", mm(full(6), c["wo"][:], t1[:]))
                o.need(DV, "hn")
                o.step("mean2", mm(full(7), c["ones64"][:], hflat[:, cols(i)]))
                o.need(DV, "sq2")
                o.step("var2", mm(full(0), c["ones64"][:], sq[:]))

        @block.scalar
        def _(act):
            A = lambda out, in_, f, **k: act.activation(out, in_, f, **k)
            act.preload_act_table_set("natural_log_exp_and_others")
            act.wait_ge(s_const, 16 * len(const))
            act.wait_ge(s_set, 4)
            A(c["vec"][:, 6:8], c["vec"][:, 6:8], ACT.Copy, scale=-1.0).then_inc(s_set, 1)
            act.wait_ge(s_set, 5)
            with act.Fori(0, STEPS) as i:
                o = On(act, AC, i)
                full = lambda b: bank[b][:, 0:NCOL]

                def rstd(src, eps, pe_step, a, b):
                    o.need(PE, pe_step)
                    o.step(a, A(rs[:], full(src), ACT.Ln, bias=eps))
                    o.need(AC, a)
                    o.step(b, A(rs[:], rs[:], ACT.Exp, scale=-0.5))

                rstd(1, cst[:, 0:1], "var", "lnv", "rstd")
                o.need(PE, "hw")
                o.step("ew", A(t1[:], full(3), ACT.Exp, scale=2.0))
                o.need(PE, "ha")
                o.step("hac", A(ha[:], full(4), ACT.Copy))
                o.need(PE, "vF")
                o.step("vFc", A(vF[:], full(6), ACT.Copy))
                o.need(PE, "vN")
                o.step("VN", A(VN[:].rearrange("p k f -> p (k f)"), bank[7][0:TL, :], ACT.Copy))
                for b in range(2):
                    o.need(PE, "hg%d" % b)
                    o.step("eg%d" % b, A(gh[:, b, :], full(b), ACT.Exp, scale=-1.0))
                o.need(PE, "w")
                o.step("ew2", A(t2[:], full(3), ACT.Exp, scale=-1.0, bias=vec("b_w")))
                o.need(PE, "a")
                o.step("ea", A(aa[:], full(4), ACT.Exp, scale=-1.0, bias=vec("b_a")))
                o.need(DV, "ssm")
                o.step("lnk", A(rs[:], sq[:], ACT.Ln, scale=float(2 ** 30)))
                o.need(AC, "lnk")
                o.step("rk", A(rs[:], rs[:], ACT.Exp, scale=-0.5, bias=cst[:, 2:3]))
                o.need(DV, "cs")
                o.step("Pi", A(Pi[:], cs[:], ACT.Exp))
                o.step("Pn", A(Pn[:], cs[:], ACT.Exp, scale=-1.0))
                o.need(DV, "ce")
                o.step("Pe", A(Pe[:], ww[:], ACT.Exp))
                o.need(PE, "tA")
                o.step("aN", A(Y[:, :, :, 0:D], bank[6][0:TL, :].rearrange("p (k b f) -> p k b f", b=2, f=D), ACT.Copy))
                o.need(PE, "tB")
                o.step("bN", A(bN[:].rearrange("p k f -> p (k f)"), bank[7][0:TL, :], ACT.Copy))
                o.need(PE, "tK")
                o.step("kN", A(kN[:].rearrange("p k f -> p (k f)"), bank[2][0:TL, :], ACT.Copy))
                o.need(PE, "LKV")
                o.step("LKV", A(Y[:, :, :, D:P], bank[5][0:TL, :].rearrange("p (k b f) -> p k b f", b=2, f=D), ACT.Copy))
                for name, b0 in (("N2T", 3), ("N2", 0), ("N4T", 3), ("N4", 0), ("N8T", 3)):
                    o.need(PE, name)
                    for h in range(2):
                        ins = A(mats[name][:, 4 * h:4 * h + 4, :], unit4(b0 + h), ACT.Copy)
                    o.step(name, ins)
                o.need(PE, "g")
                o.step("gF", A(gF[:], full(0), ACT.Copy))
                o.need(PE, "O")
                for k in range(NT_):
                    ins = A(oF[:, TL * k:TL * k + TL], bank[3 + k][:, 0:TL], ACT.Copy)
                o.step("oF", ins)
                rstd(5, cst[:, 1:2], "ovar", "lno", "rstdo")
                rstd(0, cst[:, 0:1], "var2", "lnv2", "rstd2")

        @block.vector
        def _(v):
            v.wait_ge(s_const, 16 * len(const))
            v.wait_ge(s_h, 16 * PAIRS)
            v.wait_ge(s_set, 5)
            v.memset(xp[:], 0.0).then_inc(s_set, 1)
            v.wait_ge(s_set, 6)
            with v.Fori(0, STEPS) as i:
                o = On(v, DV, i)
                tt, st, ts = v.tensor_tensor, v.scalar_tensor_tensor, v.tensor_scalar
                full = lambda b: bank[b][:, 0:NCOL]

                def own(*names):
                    o.need(DV, *names)

                def layer_center(b, pe_step, a, s):
                    o.need(PE, pe_step)
                    o.step(a, tt(xc[:], hflat[:, cols(i)], full(b), ALU.subtract))
                    own(a)
                    o.step(s, tt(sq[:], xc[:], xc[:], ALU.mult))

                layer_center(0, "mean", "xc", "sq")
                o.need(AC, "rstd")
                o.step("x", tt(xp[:, :, 1:TK + 1], pr(xc), pr(rs), ALU.mult))
                own("x")
                o.step("dx", tt(pr(dx), xp[:, :, 0:TK], xp[:, :, 1:TK + 1], ALU.subtract))
                own("dx")
                for m in ("k", "w", "a", "r", "v", "g"):
                    o.step("mix_" + m, st(pr(xm[m]), pr(dx), vec("mix_" + m), xp[:, :, 1:TK + 1], ALU.mult, ALU.add))

                def one_over_one_plus(t, a, b):
                    o.step(a, ts(t, t, 1.0, None, ALU.add))
                    own(a)
                    o.step(b, v.reciprocal(t, t))

                o.need(AC, "ew")
                one_over_one_plus(t1[:], "w1", "w2")
                own("w2")
                o.step("w3", ts(t1[:], t1[:], -2.0, 1.0, ALU.mult, ALU.add))
                o.need(AC, "ew2")
                one_over_one_plus(t2[:], "s1", "s2")
                own("s2")
                o.step("s3", ts(ww[:], t2[:], DECAY, None, ALU.mult))
                o.need(AC, "ea")
                one_over_one_plus(aa[:], "a1", "a2")
                o.need(PE, "k")
                o.step("kk", ts(kk[:], full(2), vec("k_k"), None, ALU.mult))
                own("kk")
                o.step("kk2", tt(sq[:], kk[:], kk[:], ALU.mult))
                o.need(PE, "ss")
                o.step("ssm", ts(sq[:], full(1), 1e-24, None, ALU.max))
                o.need(AC, "rk")
                o.step("kkn", tt(kk[:], kk[:], rs[:], ALU.mult))
                own("a2")
                o.step("ka1", ts(t2[:], aa[:], 1.0, vec("k_a"), ALU.subtract, ALU.mult))
                own("ka1")
                o.step("kp", st(kp[:], t2[:], 1.0, full(2), ALU.add, ALU.mult))
                own("kkn")
                o.step("b", tt(bb[:], kk[:], aa[:], ALU.mult))
                own("s3")
                o.step("cs", v.tensor_tensor_scan(cs[:], c["smask"][:], ww[:], 0.0, ALU.mult, ALU.add))
                own("cs")
                o.step("ce", tt(ww[:], cs[:], ww[:], ALU.subtract))
                o.need(AC, "Pe")
                o.step("al", tt(al[:], kk[:], Pe[:], ALU.mult))
                own("b")
                o.step("be", tt(be[:], bb[:], Pn[:], ALU.mult))
                o.step("ka", tt(ka[:], kp[:], Pn[:], ALU.mult))
                o.need(PE, "r")
                o.step("rho", tt(rho[:], full(5), Pi[:], ALU.mult))
                o.step("rk", st(rk[:], full(5), vec("r_k"), kp[:], ALU.mult, ALU.mult))
                o.need(PE, "bsum")
                o.need(AC, "vFc")
                o.step("bon", tt(bon[:], full(5), vF[:], ALU.mult))
                o.need(AC, "eg1")
                gv = gh[:].rearrange("p b t -> p (b t)")
                o.step("g", ts(gv, gv, 1.0, None, ALU.add))

                def gate_part(k):
                    n = 2 * NCOL // 8
                    own("g")
                    o.step("g%d" % k, v.reciprocal(gv[:, n * k:n * k + n], gv[:, n * k:n * k + n]))

                for part, (name, pe_step, b0, mask) in enumerate((("NT", "LT", 3, "m_lt"), ("N", "L", 0, "m_l"), ("KA", "KA", 3, "m_ka"),
                                                ("KR", "KR", 0, "m_kr"), ("BR", "BR", 3, "m_br"))):
                    o.need(PE, pe_step)
                    for h in range(2):
                        ins = tt(mats[name][:, 4 * h:4 * h + 4, :], unit4(b0 + h),
                                 c[mask][:].unsqueeze(1).to_broadcast([TL, 4, TL]), ALU.mult)
                    o.step(name, ins)
                    gate_part(part)
                o.need(AC, "LKV")
                for n in range(1, 5):
                    for h, x in enumerate("ab"):
                        o.need(PE, "Y%d%s" % (n, x))
                        if n > 1:
                            own("Y%d%s" % (n - 1, x))
                        yv = Y[:, 2 * h:2 * h + 2].rearrange("p k b f -> p (k b f)")
                        o.step("Y%d%s" % (n, x), tt(yv, yv, bank[6 + h][0:TL, :], ALU.add))
                    if n < 4:
                        gate_part(4 + n)
                own("Y4b")
                for k in range(NT_):
                    ins = tt(uX[:, k], Y[:, k, :, D:P].unsqueeze(2).to_broadcast([TL, 2, CT, D]),
                             c["cmn"][:].unsqueeze(1).unsqueeze(3).to_broadcast([TL, 2, CT, D]), ALU.mult)
                o.step("uX", ins)
                for k in range(NT_):
                    o.need(PE, "GT%d" % k)
                    o.step("GT%d" % k, st(GT[:, k, :], full(k), -1.0, c["eye6"][:], ALU.mult, ALU.add))
                pend = pr(Pi)[:, :, CH - 1:TK:CH]
                for k in range(NT_):
                    o.need(PE, "HP%d" % k)
                    o.step("HP%d" % k, v.tensor_copy(HP[:, k, :], full(4 + k)))
                o.need(PE, "RT")
                o.step("RT", tt(al[:], rho[:], full(0), ALU.add))
                own("HP3")
                hv = HP[:].rearrange("p (a h) (c f) -> p a h c f", h=2, f=D)
                o.step("M1", tt(M[:, 1], hv[:, :, 0, 0, :], pend[:, :, 0:1].to_broadcast([P, GP, D]), ALU.mult))
                for ci in range(2, NC):
                    o.need(PE, "M%d" % ci)
                    o.step("M%d" % ci, tt(M[:, ci], bank[1 + (ci - 1) % 2][:, 0:GP * D]
                                          .rearrange("p (a f) -> p a f", f=D),
                                          pend[:, :, ci - 1:ci].to_broadcast([P, GP, D]), ALU.mult))
                o.need(PE, "omean")
                o.step("oc", tt(oc[:], oF[:], full(4), ALU.subtract))
                own("oc")
                o.step("osq", tt(sq[:], oc[:], oc[:], ALU.mult))
                o.need(AC, "rstdo")
                o.step("on1", tt(t1[:], oc[:], rs[:], ALU.mult))
                own("on1")
                o.step("on2", ts(t1[:], t1[:], vec("gn_w"), vec("gn_b"), ALU.mult, ALU.add))
                own("on2")
                o.step("on3", tt(t1[:], t1[:], bon[:], ALU.add))
                own("on3")
                o.step("on4", tt(t1[:], t1[:], gF[:], ALU.mult))
                o.need(PE, "out")
                o.step("hn", tt(hflat[:, cols(i)], hflat[:, cols(i)], full(6), ALU.add))
                own("hn")
                layer_center(7, "mean2", "xc2", "sq2")
                o.need(AC, "rstd2")
                o.step("x2", tt(xflat[:, cols(i)], xc[:], rs[:], ALU.mult))


def expert_phase(nc, ctx, W, hall, x2all, out):
    sb = lambda n, s, d=F32: ctx.enter_context(nc.sbuf_tensor(n, s, d))
    sem = lambda n: ctx.enter_context(nc.semaphore(n))
    bank = [ctx.enter_context(nc.psum_tensor(f"fbank{k}", [P, 512], F32)) for k in range(8)]
    names = ("fw1", "fw2", "fwo", "fwr", "fbr", "fbo", "fsel", "fbn", "ident")
    c = {k: sb("f_" + k, list(W[k].shape), F32) for k in names}
    eps = sb("f_eps", [P, 1])
    sc = sb("f_sc", [P, 2, EJ])
    bi = sb("f_bi", [P, 2, EJ])
    fs = sb("f_sum", [P, TK])
    lg, ex = (sb(n, [TL, 2, EXPERTS]) for n in ("f_lg", "f_ex"))
    mx, su = (sb(n, [TL, 2, 1]) for n in ("f_mx", "f_su"))
    wT = sb("f_wT", [EXPERTS, TK])
    wb = sb("f_wb", [P, EJ, TK])
    bw = sb("f_bw", [P, TK])
    H1 = sb("f_h1", [P, 4, NCOL])
    H2 = sb("f_h2", [P, 4, NCOL])
    fo = sb("f_out", [P, 2, NCOL])
    s = {n: sem("f_" + n) for n in ("const", "eps", "bn", "rt", "route", "table", "mm1", "h1", "mm2", "h2", "wgt",
                                    "mm3", "res", "store")}
    hflat = hall[:].rearrange("p a t -> p (a t)")
    xflat = x2all[:].rearrange("p a t -> p (a t)")
    M2 = (4, 5, 7)
    BN = lambda what: c["fbn"][:, :, what, :]
    U = 2 * EJ

    with nc.Block() as block:
        @block.sync
        def _(sp):
            for k in names:
                sp.dma_start(c[k][:], W[k]).then_inc(s["const"], 16)
            sp.dma_start(fo[:, 1, 1:P + 1], W["ident"]).then_inc(s["store"], 16)
            with sp.Fori(0, STEPS) as i:
                sp.wait_ge(s["res"], 2 * i + 3)
                sp.wait_ge(s["const"], 16 * len(names))
                for p in range(GP):
                    src = i * GP + p
                    sp.dma_start(out[bass.ds(src, 1), :, :].rearrange("o p t -> p (o t)"),
                                 fo[:, 0, TK * p:TK * p + TR]).then_inc(s["store"], 16)
            sp.wait_ge(s["store"], 16 * (PAIRS + 1))

        @block.scalar
        def _(act):
            act.preload_act_table_set("natural_log_exp_and_others")
            act.wait_ge(s["const"], 16 * len(names))
            act.wait_ge(s["eps"], 1)
            for l in range(2):
                act.activation(sc[:, l], BN(4)[:, l], ACT.Ln, bias=eps[:, 0:1]).then_inc(s["table"], 1)
            act.wait_ge(s["table"], 2)
            act.activation(sc[:], sc[:], ACT.Exp, scale=-0.5).then_inc(s["table"], 1)
            act.wait_ge(s["rt"], 4)
            act.activation(ex[:], lg[:], ACT.Exp).then_inc(s["table"], 1)
            act.wait_ge(s["bn"], 4)
            with act.Fori(0, STEPS) as i:
                act.wait_ge(s["res"], 2 * i + 1)
                for u in range(U + 2):
                    if u < U:
                        act.wait_ge(s["mm1"], i * U + u + 1)
                        if u >= 4:
                            act.wait_ge(s["mm2"], i * U + u - 3)
                        act.activation(H1[:, u % 4, :], bank[u % 4][:, 0:NCOL], ACT.Relu,
                                       scale=sc[:, 0, u // 2:u // 2 + 1], bias=bi[:, 0, u // 2:u // 2 + 1])\
                            .then_inc(s["h1"], 1)
                    if u >= 2:
                        w = u - 2
                        act.wait_ge(s["mm2"], i * U + w + 1)
                        if w >= 4:
                            act.wait_ge(s["mm3"], i * U + w - 3)
                        act.activation(H2[:, w % 4, :], bank[M2[w % 3]][:, 0:NCOL], ACT.Relu,
                                       scale=sc[:, 1, w // 2:w // 2 + 1], bias=bi[:, 1, w // 2:w // 2 + 1])\
                            .then_inc(s["h2"], 1)

        @block.tensor
        def _(pe):
            mm = lambda out, l, r, a=True, z=True: pe.matmul(out, l, r, start=a, stop=z)
            pe.wait_ge(s["const"], 16 * len(names))
            pe.wait_ge(s["rt"], 1)
            for h in range(2):
                ins = mm(bank[7][0:TL, 8 * h:8 * h + 8], fs[:, TL * h:TL * h + TL], c["fwr"][:])
            ins.then_inc(s["route"], 1)
            pe.wait_ge(s["rt"], 7)
            for h in range(2):
                ins = pe.transpose(bank[6][0:EXPERTS, TL * h:TL * h + TL], ex[:, h, :], c["ident"][0:TL, 0:TL])
            ins.then_inc(s["route"], 1)
            pe.wait_ge(s["rt"], 8)
            for j in range(EJ):
                ins = mm(bank[j][:, 0:TK], c["fsel"][:, j, :], wT[:])
            ins.then_inc(s["route"], 1)
            mm(bank[5][:, 0:TK], c["fbo"][:], wT[:]).then_inc(s["route"], 1)
            pe.wait_ge(s["rt"], 10)
            with pe.Fori(0, STEPS) as i:
                for u in range(U + 3):
                    if u < U:
                        j, b = divmod(u, 2)
                        if u >= 4:
                            pe.wait_ge(s["h1"], i * U + u - 3)
                        mm(bank[u % 4][:, 0:NCOL], c["fw1"][:, b, j, :], xflat[:, bass.ds(i * NCOL, NCOL)])\
                            .then_inc(s["mm1"], 1)
                    if 1 <= u <= U:
                        w = u - 1
                        pe.wait_ge(s["h1"], i * U + w + 1)
                        if w >= 3:
                            pe.wait_ge(s["h2"], i * U + w - 2)
                        mm(bank[M2[w % 3]][:, 0:NCOL], c["fw2"][:, w // 2, :], H1[:, w % 4, :]).then_inc(s["mm2"], 1)
                    if u >= 3:
                        w = u - 3
                        j, b = divmod(w, 2)
                        if w == 0:
                            pe.wait_ge(s["res"], 2 * i + 1)
                        pe.wait_ge(s["wgt"], i * U + w + 1)
                        mm(bank[6][64 * b:64 * b + 64, 0:NCOL], c["fwo"][:, j, :], H2[:, w % 4, :], j == 0,
                           j == EJ - 1).then_inc(s["mm3"], 1)

        @block.vector
        def _(v):
            tt = v.tensor_tensor
            v.memset(eps[:], 1e-3).then_inc(s["eps"], 1)
            v.memset(fo[:, 1, 0:1], 0.0).then_inc(s["res"], 1)
            v.tensor_reduce(fs[:], x2all[:].rearrange("p a t -> p t a"), axis=AX_X, op=ALU.add).then_inc(s["rt"], 1)
            v.wait_ge(s["const"], 16 * len(names))
            v.wait_ge(s["route"], 1)
            v.scalar_tensor_tensor(lg[:], bank[7][0:TL, 0:16].rearrange("p (h e) -> p h e", h=2), 1.0 / (2 * PAIRS),
                                   c["fbr"][:], ALU.mult, ALU.add).then_inc(s["rt"], 1)
            v.wait_ge(s["rt"], 2)
            v.tensor_reduce(mx[:], lg[:], axis=AX_X, op=ALU.max).then_inc(s["rt"], 1)
            v.wait_ge(s["rt"], 3)
            tt(lg[:], lg[:], mx[:].to_broadcast([TL, 2, EXPERTS]), ALU.subtract).then_inc(s["rt"], 1)
            v.wait_ge(s["table"], 3)
            tt(sc[:], sc[:], BN(1), ALU.mult).then_inc(s["bn"], 1)
            tt(bi[:], BN(0), BN(3), ALU.subtract).then_inc(s["bn"], 1)
            v.wait_ge(s["bn"], 2)
            tt(bi[:], bi[:], sc[:], ALU.mult).then_inc(s["bn"], 1)
            v.wait_ge(s["bn"], 3)
            tt(bi[:], bi[:], BN(2), ALU.add).then_inc(s["bn"], 1)
            v.wait_ge(s["table"], 4)
            v.tensor_reduce(su[:], ex[:], axis=AX_X, op=ALU.add).then_inc(s["rt"], 1)
            v.wait_ge(s["rt"], 5)
            v.reciprocal(su[:], su[:]).then_inc(s["rt"], 1)
            v.wait_ge(s["rt"], 6)
            tt(ex[:], ex[:], su[:].to_broadcast([TL, 2, EXPERTS]), ALU.mult).then_inc(s["rt"], 1)
            v.wait_ge(s["route"], 2)
            v.tensor_copy(wT[:], bank[6][0:EXPERTS, 0:TK]).then_inc(s["rt"], 1)
            v.wait_ge(s["route"], 4)
            for j in range(EJ):
                ins = v.tensor_copy(wb[:, j, :], bank[j][:, 0:TK])
            ins.then_inc(s["rt"], 1)
            v.tensor_copy(bw[:], bank[5][:, 0:TK]).then_inc(s["rt"], 1)
            v.wait_ge(s["rt"], 10)
            with v.Fori(0, STEPS) as i:
                for w in range(U):
                    h2 = H2[:, w % 4, :].rearrange("p (a t) -> p a t", t=TK)
                    v.wait_ge(s["h2"], i * U + w + 1)
                    tt(h2, h2, wb[:, w // 2, :].unsqueeze(1).to_broadcast([P, GP, TK]), ALU.mult)\
                        .then_inc(s["wgt"], 1)
                v.wait_ge(s["mm3"], i * U + U)
                v.wait_ge(s["store"], i * 16 * GP + 16)
                tt(fo[:, 0, :], hflat[:, bass.ds(i * NCOL, NCOL)], bank[6][:, 0:NCOL], ALU.add).then_inc(s["res"], 1)
                v.wait_ge(s["res"], 2 * i + 2)
                f3 = fo[:, 0, :].rearrange("p (a t) -> p a t", t=TK)
                tt(f3, f3, bw[:].unsqueeze(1).to_broadcast([P, GP, TK]), ALU.add).then_inc(s["res"], 1)


def build(nc, d, hid, out):
    with ExitStack() as ctx:
        ssm_phase(nc, ctx, d["xT"], d["alog"], d["Dp"], d["Wb"], d["Wc"], d["Wr"], d["Wdt"], d["bdt"],
                  d["sel"], d["zsel"], hid)
    with ExitStack() as outer:
        hall = outer.enter_context(nc.sbuf_tensor("hall", [P, PAIRS, TK], F32))
        x2all = outer.enter_context(nc.sbuf_tensor("x2all", [P, PAIRS, TK], F32))
        with ExitStack() as ctx:
            mixer_phase(nc, ctx, d, hid, hall, x2all)
        with ExitStack() as ctx:
            expert_phase(nc, ctx, d, hall, x2all, out)


def layout(I):
    import numpy as np
    f = np.float32
    out = {}
    out["xT"] = np.ascontiguousarray(I["x"].reshape(32, 2, 750, 64).transpose(0, 1, 3, 2).reshape(32, 128, 750))

    def two(m):
        z = np.zeros((128, 128), f)
        z[0:64, 0:64] = m
        z[64:128, 64:128] = m
        return z

    W = I["L0_tok_W_dbc"]
    out["Wr"] = np.stack([two(np.repeat(W[l, 0:1, :].T, 64, 1)) for l in range(3)], 1)
    out["Wb"] = np.stack([two(W[l, 1:65, :].T) for l in range(3)], 1)
    out["Wc"] = np.stack([two(W[l, 65:129, :].T) for l in range(3)], 1)
    al = I["L0_tok_A_log"].transpose(2, 0, 1)
    out["alog"] = np.concatenate([al, al], 0)
    for k, s in (("Dp", "L0_tok_D"), ("bdt", "L0_tok_b_dt")):
        out[k] = np.concatenate([I[s].T, I[s].T], 0)
    w = I["L0_tok_W_dt"][:, :, 0].T
    out["Wdt"] = np.concatenate([w, w], 0)
    sel = np.zeros((3, 2, 16, 16, 2, 64), f)
    for b in range(2):
        for e in range(16):
            sel[:, b, e, e, b, :] = 1
    out["sel"] = sel.reshape(96, 16, 128)
    z = np.zeros((16, 8, 8, 67), f)
    for e in range(16):
        for q in range(8):
            z[e, q, q, 3 + 4 * e] = 0.5
    out["zsel"] = z.reshape(128, 8, 67)
    one = np.zeros((128, 128), f)
    one[0:64, 0:64] = one[64:, 64:] = 1
    out["ones"] = one
    out["ones64"] = one / np.float32(64)
    out["ident"] = np.eye(128, dtype=f)
    for k, n in (("wk", "W_k"), ("ww", "A_w"), ("wa", "A_a"), ("wr_", "W_r"), ("wv", "W_v"), ("wbw", "B_w"),
                 ("wba", "B_a"), ("wo", "W_o")):
        out[k] = two(I["L0_attn_" + n])
    out["wg"] = np.concatenate([I["L0_attn_A_g"]] * 2, 0)
    out["wbg"] = I["L0_attn_B_g"]
    vecs = list(I["L0_attn_x_mix"]) + [I["L0_attn_" + n] for n in ("b_w", "b_a", "k_k", "k_a", "r_k", "gn_w", "gn_b")]
    out["vec"] = np.concatenate([np.stack(vecs, 1)] * 2, 0)
    t = np.arange(96)
    same = (t[:, None] // 16 == t[None, :] // 16)
    before = same & (t[:, None] < t[None, :])
    upto = same & (t[:, None] <= t[None, :])
    out["m_lt"], out["m_l"] = -before.astype(f), -before.T.astype(f)
    out["m_ka"], out["m_kr"], out["m_br"] = before.astype(f), upto.astype(f), -upto.astype(f)
    out["cm"] = (t[:, None] // 16 == np.arange(6)[None, :]).astype(f)
    out["cmn"] = -out["cm"]
    e64 = np.eye(64, dtype=f)
    out["eye6"] = np.tile(e64, (2, 6))
    out["smask"] = np.tile((np.arange(384) % 16 != 0).astype(f), (128, 1))

    def ffn(n):
        return I["L0_ffn_" + n]

    w1 = np.zeros((128, 2, 4, 128), f)
    w2 = np.zeros((128, 4, 128), f)
    for j in range(4):
        for h in range(2):
            for b in range(2):
                w1[64 * b:64 * b + 64, b, j, 64 * h:64 * h + 64] = ffn("W1")[2 * j + h]
            w2[64 * h:64 * h + 64, j, 64 * h:64 * h + 64] = ffn("W2")[2 * j + h]
    out["fw1"], out["fw2"] = w1, w2
    out["fwo"] = ffn("Wo").reshape(4, 128, 64).transpose(1, 0, 2)
    out["fwr"] = np.concatenate([ffn("Wr")] * 2, 0)
    out["fbr"] = np.broadcast_to(ffn("br"), (96, 2, 8))
    out["fbo"] = np.concatenate([ffn("bo")] * 2, 1)
    fsel = np.zeros((8, 4, 2, 64), f)
    for j in range(4):
        for h in range(2):
            fsel[2 * j + h, j, h] = 1
    out["fsel"] = fsel.reshape(8, 4, 128)
    out["fbn"] = np.stack([np.stack([ffn(n + l).reshape(4, 128).T for n in ("b", "g", "be", "m", "v")], 1)
                           for l in "12"], 1)
    return {k: np.ascontiguousarray(v) for k, v in out.items()}


def kernel(**inputs):
    import numpy as np
    import concourse.bacc as bacc
    from concourse.bass_utils import run_bass_kernel_spmd as run
    nc = bacc.Bacc("TRN2", target_bir_lowering=False, num_devices=1)
    arrays = layout({k: np.asarray(v) for k, v in inputs.items()})
    d = {k: nc.dram_tensor("in_" + k, a.shape, mybir.dt.from_np(a.dtype), kind="ExternalInput").ap()
         for k, a in arrays.items()}
    hid = nc.dram_tensor("hidden", (32, 128, 187), F32, kind="Internal").ap()
    o = nc.dram_tensor("out_0", (32, 128, 187), F32, kind="ExternalOutput").ap()
    build(nc, d, hid, o)
    r = run(nc, [{"in_" + k: a for k, a in arrays.items()}], core_ids=[0])
    y = r.results[0]["out_0"]
    return np.ascontiguousarray(y.reshape(32, 2, 64, 187).transpose(0, 1, 3, 2).reshape(64, 187, 64))
```
